# Optimizing a Trainium2 kernel written in Bass

```python
import numpy as np
import jax
import jax.numpy as jnp

def _softmax(x, axis=-1):
    return jax.nn.softmax(x, axis=axis)

def _gelu(x):
    return jax.nn.gelu(x, approximate=True)

def _silu(x):
    return jax.nn.silu(x)

def _sigmoid(x):
    return jax.nn.sigmoid(x)

def _layernorm(x, axis=-1, eps=1e-05):
    m = jnp.mean(x, axis=axis, keepdims=True)
    v = jnp.var(x, axis=axis, keepdims=True)
    return (x - m) / jnp.sqrt(v + eps)

def _scatter_add(tgt, idx, src, axis=0):
    return tgt.at[idx].add(src)

def _segment_sum(src, seg, n):
    return jax.ops.segment_sum(src, seg, n)
kernel_name = 'mk_adaln_ffn_d1_seqx_r8_79b45e'

def setup_inputs(seed: int=0):
    np.random.seed(seed)
    _w = jnp.asarray

    def _rec_inputs():
        import jax
        import jax.numpy as jnp
        _rk = jax.random.key(seed)
        x = 7.22e-05 + 1 * jax.random.normal(jax.random.fold_in(_rk, 1), (128, 32, 512), jnp.float32)
        _lenS = 32 - jax.random.randint(jax.random.fold_in(_rk, 7), (128,), 0, max(1, 32 // 4) + 1, jnp.int32)
        _lenS2 = 32 - jax.random.randint(jax.random.fold_in(_rk, 8), (128,), 0, max(1, 32 // 4) + 1, jnp.int32)
        itok_B_2_6 = jax.random.randint(jax.random.fold_in(_rk, 11), (128,), 2, 7, jnp.int32)
        return (x, itok_B_2_6)
    x, itok_B_2_6 = _rec_inputs()

    def _L0_cond_setup():
        import jax, jax.numpy as jnp
        import numpy as np
        B, N, H, F = (4, 64, 512, 1376)
        L, R, RANK = (1, 16, 16)
        SCALE = 0.5
        key = jax.random.key(seed)
        ks = jax.random.split(key, 12)
        nrm = lambda k, shape, fan: jax.random.normal(k, shape, jnp.float32) * fan ** (-0.5)
        inp = {'x': jax.random.normal(ks[0], (B, N, H), jnp.float32), 'W_gate': nrm(ks[1], (F, H), H), 'W_up': nrm(ks[2], (F, H), H), 'W_down': nrm(ks[3], (H, F), F), 'A_gate': nrm(ks[4], (L, R, RANK, H), H), 'B_gate': nrm(ks[5], (L, R, F, RANK), RANK), 'A_up': nrm(ks[6], (L, R, RANK, H), H), 'B_up': nrm(ks[7], (L, R, F, RANK), RANK), 'A_down': nrm(ks[8], (L, R, RANK, F), F), 'B_down': nrm(ks[9], (L, R, H, RANK), RANK), 'lora_indices': jax.random.randint(ks[10], (B,), 0, R), 'layer_idx': 0}
        return inp
    _L0_cond_all = _L0_cond_setup()
    _L0_cond_in = {k: v for k, v in _L0_cond_all.items() if k in ('W_gate', 'W_up', 'W_down', 'A_gate', 'B_gate', 'A_up', 'B_up', 'A_down', 'B_down')}
    del _L0_cond_all

    def _L0_ffn_setup():
        import jax, jax.numpy as jnp
        import numpy as np
        QUANT_LEVELS = jnp.array([-1.5, -0.5, 0.5, 1.5], dtype=jnp.float32)
        EPS = 1e-05
        key = jax.random.key(seed)
        k1, k2, k3 = jax.random.split(key, 3)
        B, S, D_IN, D_OUT = (4, 256, 512, 512)
        x = jax.random.normal(k1, (B, S, D_IN), dtype=jnp.float32)
        weight_2bit = jax.random.randint(k2, (D_OUT, D_IN), 0, 4, dtype=jnp.int32)
        weight_scale = jnp.ones((1,), dtype=jnp.float32)
        bias = jax.random.normal(k3, (D_OUT,), dtype=jnp.float32)
        return {'x': x, 'weight_2bit': weight_2bit, 'weight_scale': weight_scale, 'bias': bias}
    _L0_ffn_all = _L0_ffn_setup()
    _L0_ffn_in = {k: v for k, v in _L0_ffn_all.items() if k in ('weight_2bit', 'weight_scale', 'bias')}
    del _L0_ffn_all
    return {'x': x, 'itok_B_2_6': itok_B_2_6, 'L0_cond_W_gate': _L0_cond_in['W_gate'], 'L0_cond_W_up': _L0_cond_in['W_up'], 'L0_cond_W_down': _L0_cond_in['W_down'], 'L0_cond_A_gate': _L0_cond_in['A_gate'], 'L0_cond_B_gate': _L0_cond_in['B_gate'], 'L0_cond_A_up': _L0_cond_in['A_up'], 'L0_cond_B_up': _L0_cond_in['B_up'], 'L0_cond_A_down': _L0_cond_in['A_down'], 'L0_cond_B_down': _L0_cond_in['B_down'], 'L0_ffn_weight_2bit': _L0_ffn_in['weight_2bit'], 'L0_ffn_weight_scale': _L0_ffn_in['weight_scale'], 'L0_ffn_bias': _L0_ffn_in['bias']}

def reference(x, itok_B_2_6, L0_cond_W_gate, L0_cond_W_up, L0_cond_W_down, L0_cond_A_gate, L0_cond_B_gate, L0_cond_A_up, L0_cond_B_up, L0_cond_A_down, L0_cond_B_down, L0_ffn_weight_2bit, L0_ffn_weight_scale, L0_ffn_bias):
    import jax
    import jax.numpy as jnp

    def _L0_cond_ref(x, W_gate, W_up, W_down, A_gate, B_gate, A_up, B_up, A_down, B_down, lora_indices, layer_idx):
        import jax, jax.numpy as jnp
        import numpy as np
        B, N, H, F = (4, 64, 512, 1376)
        L, R, RANK = (1, 16, 16)
        SCALE = 0.5

        def lora_add(base, inp, A, B):
            Ab = A[layer_idx][lora_indices]
            Bb = B[layer_idx][lora_indices]
            t = jnp.einsum('bri,bni->bnr', Ab, inp)
            return base + jnp.einsum('bor,bnr->bno', Bb, t) * SCALE
        gate = lora_add(jnp.einsum('bnh,fh->bnf', x, W_gate), x, A_gate, B_gate)
        up = lora_add(jnp.einsum('bnh,fh->bnf', x, W_up), x, A_up, B_up)
        act = jax.nn.silu(gate) * up
        down = lora_add(jnp.einsum('bnf,hf->bnh', act, W_down), act, A_down, B_down)
        return down

    def _L0_ffn_ref(x, weight_2bit, weight_scale, bias):
        import jax, jax.numpy as jnp
        import numpy as np
        QUANT_LEVELS = jnp.array([-1.5, -0.5, 0.5, 1.5], dtype=jnp.float32)
        EPS = 1e-05
        x_abs_max = jnp.clip(jnp.max(jnp.abs(x), axis=-1, keepdims=True), EPS)
        x_norm = x / x_abs_max
        weight_float = QUANT_LEVELS[weight_2bit]
        out = jnp.einsum('bsd,od->bso', x_norm, weight_float)
        out = out * (x_abs_max * weight_scale)
        out = out + bias
        return out
    x = x + _L0_ffn_ref(_L0_cond_ref(x, L0_cond_W_gate, L0_cond_W_up, L0_cond_W_down, L0_cond_A_gate, L0_cond_B_gate, L0_cond_A_up, L0_cond_B_up, L0_cond_A_down, L0_cond_B_down, itok_B_2_6, 0), L0_ffn_weight_2bit, L0_ffn_weight_scale, L0_ffn_bias)
    return x

_drawn_inputs = setup_inputs


def setup_inputs(seed=0):
    import zlib

    import numpy as np

    out = dict(_drawn_inputs(seed))
    spreads = {}
    factors = {}
    for name, (base, spread) in spreads.items():
        noise = np.random.default_rng([zlib.crc32(name.encode()), seed]).standard_normal(out[name].shape)
        drawn = base * np.exp(spread * noise) if base else spread * noise
        out[name] = jnp.asarray(drawn.astype(out[name].dtype))
    for name, factor in factors.items():
        out[name] = (out[name] * factor).astype(out[name].dtype)
    return out
```

```python
from contextlib import ExitStack

import numpy as np

import concourse.bass as bass
from concourse import mybir

F32 = mybir.dt.float32
F32R = mybir.dt.float32r
I32 = mybir.dt.int32
ALU = mybir.AluOpType
ACT = mybir.ActivationFunctionType
AX_X = mybir.AxisListType.X

P = 128
TOKENS = 4096
SEQ = 32
TILE = 256
TILES = TOKENS // TILE
ENTRIES = TILE // SEQ
SUBS = TILE // P
H = 512
KC = H // P
FF = 1376
WIDTHS = [min(P, FF - f * P) for f in range(-(-FF // P))]
FC = len(WIDTHS)
RANK = 16
LORAS = 16
SCALE = 0.5
EPS = 1e-5
AGU = 2 * KC * RANK
FIRST = 6
ROW = 2 * FF + H
PIECES = [(0, FIRST), (FIRST, FC)]


def piece_columns(piece):
    a, b = PIECES[piece]
    return 2 * a * P, 2 * min(b * P, FF)


def build(nc, x_tok, x_feat, lora_index, w_gu, w_down, w_2bit, a_gu, a_down, b_rows, scale_col, bias_rows,
          block_mask_in, identity_in, out):
    with ExitStack() as ctx:
        def sb(name, shape, dt=F32):
            return ctx.enter_context(nc.sbuf_tensor(name, shape, dt))

        def ps(name, shape):
            return ctx.enter_context(nc.psum_tensor(name, shape, F32))

        def sem(name):
            return ctx.enter_context(nc.semaphore(name))

        wgu = sb("wgu", [P, 2, 2 * FF * KC], F32R)
        wd = sb("wd", [P, 2, FC, H], F32R)
        wq = sb("wq", [P, KC, H], F32R)
        x_raw = sb("x_raw", [P, KC, TILE])
        xs = sb("xs", [P, 2, KC, TILE], F32R)
        a_raw = sb("a_raw", [P, ENTRIES, AGU])
        a_split = sb("a_split", [P, 2, KC, 2, ENTRIES, RANK], F32R)
        b_raw = sb("b_raw", [P, 2 * FF])
        b_split = sb("b_split", [P, 2, 2, 2, P], F32R)
        ad_raw = sb("ad_raw", [P, ENTRIES, FC * RANK])
        ad_split = sb("ad_split", [P, 2, 2, ENTRIES, RANK], F32R)
        bd_raw = sb("bd_raw", [P, H])
        bd_split = sb("bd_split", [P, 2, H], F32R)
        t_split = sb("t_split", [P, 2, 2, TILE], F32R)
        td_split = sb("td_split", [P, 2, TILE], F32R)
        act_full = sb("act_full", [P, 2, TILE])
        act_split = sb("act_split", [P, 2, 2, TILE], F32R)
        rows = sb("rows", [P, 3 * SUBS, H])
        norm = rows[:, 0:SUBS, :]
        x_res = rows[:, SUBS:2 * SUBS, :]
        out_rows = rows[:, 2 * SUBS:3 * SUBS, :]
        dt_split = sb("dt_split", [P, 2, KC, P], F32R)
        bias = sb("bias", [P, H])
        block_mask = sb("block_mask", [P, TILE])
        identity = sb("identity", [P, P])
        wscale = sb("wscale", [P, 1])
        amax = sb("amax", [P, SUBS])
        ones = sb("ones", [P, 1])
        rinv = sb("rinv", [P, SUBS])
        ascale = sb("ascale", [P, SUBS])
        index_sb = sb("index_sb", [1, TOKENS // SEQ], I32)
        stage_gu = rows[:, 0:4, :].rearrange("p (s a) h -> p s (a h)", s=2)
        stage_d = rows[:, 4:6, :]

        ps_down = ps("ps_down", [P, SUBS, 512])
        ps_td = ps("ps_td", [P, 512])
        ps_gate = ps("ps_gate", [P, 2, 512])
        ps_up = ps("ps_up", [P, 2, 512])
        ps_misc = ps("ps_misc", [P, 512])
        t_psum = ps_misc[:, :].rearrange("p (g t) -> p g t", g=2)
        td_psum = ps_td[:, 0:TILE]

        index_in = sem("index_in")
        ones_ready = sem("ones_ready")
        const_in = sem("const_in")
        x_in = sem("x_in")
        a_in = sem("a_in")
        b_in = [sem(f"b{n}_in") for n in range(2)]
        ad_in = [sem(f"ad{n}_in") for n in range(2)]
        bd_in = sem("bd_in")
        xres_in = sem("xres_in")
        wgu_in = [sem(f"wgu{n}_in") for n in range(2)]
        wd_in = [sem(f"wd{n}_in") for n in range(2)]
        stored = sem("stored")
        wgu_hi = sem("wgu_hi")
        wgu_lo = sem("wgu_lo")
        wd_hi = sem("wd_hi")
        wd_lo = sem("wd_lo")
        wq_ready = sem("wq_ready")
        x_hi = sem("x_hi")
        x_lo = sem("x_lo")
        a_hi = sem("a_hi")
        a_ready = sem("a_ready")
        b_hi = sem("b_hi")
        b_lo = sem("b_lo")
        ad_hi = sem("ad_hi")
        ad_ready = sem("ad_ready")
        bd_hi = sem("bd_hi")
        bd_ready = sem("bd_ready")
        t_masked = sem("t_masked")
        t_hi = sem("t_hi")
        t_lo = sem("t_lo")
        td_masked = sem("td_masked")
        td_hi = sem("td_hi")
        td_ready = sem("td_ready")
        silu_done = sem("silu_done")
        act_done = sem("act_done")
        act_hi = sem("act_hi")
        act_lo = sem("act_lo")
        amax_steps = sem("amax_steps")
        ascale_ready = sem("ascale_ready")
        norm_ready = sem("norm_ready")
        dt_hi = sem("dt_hi")
        dt_lo = sem("dt_lo")
        ffn_biased = sem("ffn_biased")
        ffn_scaled = sem("ffn_scaled")
        out_ready = sem("out_ready")
        t_done = sem("t_done")
        gate_done = sem("gate_done")
        up_done = sem("up_done")
        td_done = sem("td_done")
        down_done = sem("down_done")
        blocks_done = sem("blocks_done")
        transposed = sem("transposed")
        ffn_done = sem("ffn_done")

        def chunk_gu(f):
            return f * P * 2 * KC, 2 * KC * WIDTHS[f]

        def wgu_chunk(part, f):
            at, n = chunk_gu(f)
            return wgu[:, part, at:at + n].rearrange("p (k g w) -> p k g w", k=KC, g=2)

        block = ctx.enter_context(nc.Block())

        @block.sync
        def _(sp):
            def load_indices(tile):
                return [sp.value_load(index_sb[0:1, bass.ds(tile * ENTRIES + e, 1)], min_val=0, max_val=LORAS - 1)
                        for e in range(ENTRIES)]

            def load_x(tile):
                if not (isinstance(tile, int) and tile == 0):
                    sp.wait_ge(x_lo, tile)
                sp.dma_start(x_raw[:, :, :], x_feat[bass.ds(tile, 1), :, :, :].rearrange("a p k t -> (a p) k t")
                             ).then_inc(x_in, 16)

            def gather_a(idx):
                for e in range(ENTRIES):
                    sp.dma_start(a_raw[:, e, :], a_gu[bass.ds(idx[e], 1), :, :].rearrange("a p n -> (a p) n")
                                 ).then_inc(a_in, 16)

            def gather_pieces(idx, piece):
                a, b = piece_columns(piece)
                f0, f1 = PIECES[piece]
                for e in range(ENTRIES):
                    sp.dma_start(b_raw[e * RANK:(e + 1) * RANK, a:b],
                                 b_rows[bass.ds(idx[e], 1), :, a:b].rearrange("a r n -> (a r) n")
                                 ).then_inc(b_in[piece], 16)
                for e in range(ENTRIES):
                    sp.dma_start(ad_raw[:, e, f0 * RANK:f1 * RANK],
                                 a_down[bass.ds(idx[e], 1), :, f0 * RANK:f1 * RANK].rearrange("a p n -> (a p) n")
                                 ).then_inc(ad_in[piece], 16)

            def gather_bd(idx):
                for e in range(ENTRIES):
                    sp.dma_start(bd_raw[e * RANK:(e + 1) * RANK, :],
                                 b_rows[bass.ds(idx[e], 1), :, 2 * FF:ROW].rearrange("a r n -> (a r) n")
                                 ).then_inc(bd_in, 16)

            def load_residual(tile):
                for s in range(SUBS):
                    sp.dma_start(x_res[:, s, :], x_tok[bass.ds(tile * TILE + s * P, P), :]).then_inc(xres_in, 16)

            def load_wgu(f):
                at, n = chunk_gu(f)
                if f >= 2:
                    sp.wait_ge(wgu_lo, f - 1)
                sp.dma_start(stage_gu[:, f % 2, 0:n], w_gu[:, at:at + n]).then_inc(wgu_in[f % 2], 16)

            def load_wd(f):
                if f >= 2:
                    sp.wait_ge(wd_lo, f - 1)
                sp.dma_start(stage_d[0:WIDTHS[f], f % 2, :], w_down[f * P:f * P + WIDTHS[f], :]
                             ).then_inc(wd_in[f % 2], 16)

            def load_wq(k):
                n = FC + k
                if k < 2:
                    sp.wait_ge(wd_lo, n - 1)
                else:
                    sp.wait_ge(wq_ready, k - 1)
                sp.dma_start(stage_d[:, n % 2, :].bitcast(I32), w_2bit[:, k, :]).then_inc(wd_in[n % 2], 16)

            def store(tile):
                for s in range(SUBS):
                    sp.wait_ge(out_ready, SUBS * tile + s + 1)
                    sp.dma_start(out[bass.ds(tile * TILE + s * P, P), :], out_rows[:, s, :]).then_inc(stored, 16)

            sp.dma_start(index_sb[:, :], lora_index).then_inc(index_in, 16)
            load_x(0)
            sp.wait_ge(index_in, 16)
            idx = load_indices(0)
            gather_a(idx)
            load_wgu(0)
            sp.dma_start(block_mask[:, :], block_mask_in).then_inc(const_in, 16)
            load_wgu(1)
            gather_pieces(idx, 0)
            load_wd(0)
            load_wd(1)
            sp.dma_start(identity[:, :], identity_in).then_inc(const_in, 16)
            sp.dma_start(wscale[:, :], scale_col).then_inc(const_in, 16)
            sp.dma_start(bias[:, :], bias_rows).then_inc(const_in, 16)
            gather_pieces(idx, 1)
            gather_bd(idx)
            for f in range(2, FC):
                load_wgu(f)
                load_wd(f)
            for k in range(KC):
                load_wq(k)

            def load_tile(tile, first):
                idx = load_indices(tile)
                load_x(tile)
                sp.wait_ge(a_ready, tile)
                gather_a(idx)
                for piece in range(2):
                    sp.wait_ge(b_lo, FC * (tile - 1) + PIECES[piece][1])
                    sp.wait_ge(ad_ready, FC * (tile - 1) + PIECES[piece][1])
                    gather_pieces(idx, piece)
                    if piece == 0 and not first:
                        store(tile - 2)
                sp.wait_ge(bd_ready, tile)
                gather_bd(idx)
                if first:
                    sp.wait_ge(wq_ready, KC)
                else:
                    sp.wait_ge(stored, 16 * SUBS * (tile - 1))
                load_residual(tile - 1)

            load_tile(1, True)
            with sp.Fori(2, TILES) as tile:
                load_tile(tile, False)
            store(TILES - 2)
            sp.wait_ge(stored, 16 * SUBS * (TILES - 1))
            load_residual(TILES - 1)
            store(TILES - 1)
            sp.wait_ge(stored, 16 * SUBS * TILES)

        @block.gpsimd
        def _(pool):
            def split_a(tile):
                if not (isinstance(tile, int) and tile == 0):
                    pool.wait_ge(t_done, tile)
                pool.wait_ge(a_in, 16 * ENTRIES * (tile + 1))
                for k in range(KC):
                    raw = a_raw[:, :, k * 2 * RANK:(k + 1) * 2 * RANK].rearrange("p e (g r) -> p g e r", g=2)
                    pool.tensor_tensor(a_split[:, 0, k, :, :, :], raw,
                                       ones[:, :, None, None].to_broadcast([P, 2, ENTRIES, RANK]), ALU.mult
                                       ).then_inc(a_hi, 1)
                for k in range(KC):
                    raw = a_raw[:, :, k * 2 * RANK:(k + 1) * 2 * RANK].rearrange("p e (g r) -> p g e r", g=2)
                    pool.wait_ge(a_hi, KC * tile + k + 1)
                    last = pool.tensor_tensor(a_split[:, 1, k, :, :, :], raw,
                                              a_split[:, 0, k, :, :, :].bitcast(F32), ALU.subtract)
                last.then_inc(a_ready, 1)

            def split_bd(tile):
                if not (isinstance(tile, int) and tile == 0):
                    pool.wait_ge(blocks_done, SUBS * tile)
                pool.wait_ge(bd_in, 16 * ENTRIES * (tile + 1))
                pool.tensor_tensor(bd_split[:, 0, :], bd_raw[:, :], ones[:, :].to_broadcast([P, H]), ALU.mult
                                   ).then_inc(bd_hi, 1)
                pool.wait_ge(bd_hi, tile + 1)
                pool.tensor_tensor(bd_split[:, 1, :], bd_raw[:, :], bd_split[:, 0, :].bitcast(F32),
                                   ALU.subtract).then_inc(bd_ready, 1)

            def add_residual(tile):
                pool.wait_ge(xres_in, 16 * SUBS * (tile + 1))
                for s in range(SUBS):
                    pool.wait_ge(ffn_biased, SUBS * tile + s + 1)
                    pool.tensor_tensor(out_rows[:, s, :], x_res[:, s, :], out_rows[:, s, :], ALU.add
                                       ).then_inc(out_ready, 1)

            pool.memset(ones[:, :], 1.0).then_inc(ones_ready, 1)
            pool.wait_ge(ones_ready, 1)
            split_a(0)
            split_bd(0)
            split_a(1)
            with pool.Fori(1, TILES - 1) as tile:
                split_bd(tile)
                add_residual(tile - 1)
                split_a(tile + 1)
            split_bd(TILES - 1)
            add_residual(TILES - 2)
            add_residual(TILES - 1)

        @block.scalar
        def _(act):
            def split_hi_weights(f):
                at, n = chunk_gu(f)
                w = WIDTHS[f]
                act.wait_ge(wgu_in[f % 2], 16 * (f // 2 + 1))
                nc.scalar.activation(wgu[:, 0, at:at + n], stage_gu[:, f % 2, 0:n], ACT.Copy).then_inc(wgu_hi, 1)
                act.wait_ge(wd_in[f % 2], 16 * (f // 2 + 1))
                nc.scalar.activation(wd[0:w, 0, f, :], stage_d[0:w, f % 2, :], ACT.Copy).then_inc(wd_hi, 1)

            def split_hi_b(tile, f):
                w = WIDTHS[f]
                at = 2 * P * f
                act.wait_ge(b_in[f >= FIRST], 16 * ENTRIES * (tile + 1))
                if f >= 2:
                    act.wait_ge(up_done, FC * tile + f - 1)
                elif not (isinstance(tile, int) and tile == 0):
                    act.wait_ge(up_done, FC * tile - f)
                nc.scalar.activation(b_split[:, 0, f % 2, :, 0:w],
                                     b_raw[:, at:at + 2 * w].rearrange("p (g w) -> p g w", g=2), ACT.Copy
                                     ).then_inc(b_hi, 1)

            def normalise(tile, s):
                act.wait_ge(ascale_ready, SUBS * tile + s + 1)
                nc.scalar.activation(norm[:, s, :], ps_down[:, s, :], ACT.Copy, scale=rinv[:, s:s + 1]
                                     ).then_inc(norm_ready, 1)

            def split_hi_transposed(tile, s):
                act.wait_ge(transposed, SUBS * tile + s + 1)
                nc.scalar.activation(dt_split[:, 0, :, :], ps_misc[:, :].rearrange("p (k t) -> p k t", k=KC),
                                     ACT.Copy).then_inc(dt_hi, 1)

            def run_tile(tile, first):
                act.wait_ge(x_in, 16 * (tile + 1))
                if not first:
                    act.wait_ge(up_done, FC * tile)
                nc.scalar.activation(xs[:, 0, :, :], x_raw[:, :, :], ACT.Copy).then_inc(x_hi, 1)
                split_hi_b(tile, 0)
                if first:
                    split_hi_weights(0)
                else:
                    normalise(tile - 1, 0)
                act.wait_ge(t_masked, tile + 1)
                nc.scalar.activation(t_split[:, 0, :, :], t_psum, ACT.Copy).then_inc(t_hi, 1)
                if not first:
                    normalise(tile - 1, 1)
                for f in range(FC):
                    w = WIDTHS[f]
                    if f + 1 < FC:
                        split_hi_b(tile, f + 1)
                        if first:
                            split_hi_weights(f + 1)
                    act.wait_ge(gate_done, FC * tile + f + 1)
                    if f >= 2:
                        act.wait_ge(act_lo, FC * tile + f - 1)
                    elif not first:
                        act.wait_ge(act_lo, FC * tile - f)
                    nc.scalar.activation(act_full[0:w, f % 2, :], ps_gate[0:w, f % 2, 0:TILE], ACT.Silu
                                         ).then_inc(silu_done, 1)
                    act.wait_ge(act_done, FC * tile + f + 1)
                    nc.scalar.activation(act_split[0:w, 0, f % 2, :], act_full[0:w, f % 2, :], ACT.Copy
                                         ).then_inc(act_hi, 1)
                    if not first and f == 0:
                        split_hi_transposed(tile - 1, 0)
                    if not first and f == 2:
                        split_hi_transposed(tile - 1, 1)

            run_tile(0, True)
            with act.Fori(1, TILES) as tile:
                run_tile(tile, False)
            for s in range(SUBS):
                normalise(TILES - 1, s)
            for s in range(SUBS):
                split_hi_transposed(TILES - 1, s)

        @block.vector
        def _(dve):
            def split_lo_weights(f):
                at, n = chunk_gu(f)
                w = WIDTHS[f]
                dve.wait_ge(wgu_hi, f + 1)
                nc.vector.tensor_tensor(wgu[:, 1, at:at + n], stage_gu[:, f % 2, 0:n],
                                        wgu[:, 0, at:at + n].bitcast(F32), ALU.subtract).then_inc(wgu_lo, 1)
                dve.wait_ge(wd_hi, f + 1)
                nc.vector.tensor_tensor(wd[0:w, 1, f, :], stage_d[0:w, f % 2, :], wd[0:w, 0, f, :].bitcast(F32),
                                        ALU.subtract).then_inc(wd_lo, 1)

            def convert_wq(k):
                n = FC + k
                dve.wait_ge(wd_in[n % 2], 16 * (n // 2 + 1))
                nc.vector.tensor_scalar(wq[:, k, :], stage_d[:, n % 2, :].bitcast(I32), -1.5, None, ALU.add
                                        ).then_inc(wq_ready, 1)

            def split_lo_b(tile, f):
                w = WIDTHS[f]
                at = 2 * P * f
                dve.wait_ge(b_hi, FC * tile + f + 1)
                nc.vector.tensor_tensor(b_split[:, 1, f % 2, :, 0:w],
                                        b_raw[:, at:at + 2 * w].rearrange("p (g w) -> p g w", g=2),
                                        b_split[:, 0, f % 2, :, 0:w].bitcast(F32), ALU.subtract
                                        ).then_inc(b_lo, 1)

            def split_ad(tile, f):
                dve.wait_ge(ad_in[f >= FIRST], 16 * ENTRIES * (tile + 1))
                if f >= 2:
                    dve.wait_ge(td_done, FC * tile + f - 1)
                elif not (isinstance(tile, int) and tile == 0):
                    dve.wait_ge(td_done, FC * tile - f)
                raw = ad_raw[:, :, f * RANK:(f + 1) * RANK]
                nc.vector.tensor_copy(ad_split[:, 0, f % 2, :, :], raw).then_inc(ad_hi, 1)
                dve.wait_ge(ad_hi, FC * tile + f + 1)
                nc.vector.tensor_tensor(ad_split[:, 1, f % 2, :, :], raw, ad_split[:, 0, f % 2, :, :].bitcast(F32),
                                        ALU.subtract).then_inc(ad_ready, 1)

            def block_scales(tile, s):
                done = 2 * (SUBS * tile + s)
                dve.wait_ge(blocks_done, SUBS * tile + s + 1)
                nc.vector.tensor_reduce(amax[:, s:s + 1], ps_down[:, s, :], AX_X, ALU.max,
                                        apply_absolute_value=True).then_inc(amax_steps, 1)
                dve.wait_ge(amax_steps, done + 1)
                nc.vector.tensor_scalar(amax[:, s:s + 1], amax[:, s:s + 1], EPS, None, ALU.max
                                        ).then_inc(amax_steps, 1)
                dve.wait_ge(amax_steps, done + 2)
                nc.vector.tensor_tensor(ascale[:, s:s + 1], amax[:, s:s + 1], wscale[:, :], ALU.mult
                                        ).then_inc(ffn_scaled, 1)
                nc.vector.reciprocal(rinv[:, s:s + 1], amax[:, s:s + 1]).then_inc(ascale_ready, 1)

            def split_lo_transposed(tile, s):
                dve.wait_ge(dt_hi, SUBS * tile + s + 1)
                nc.vector.tensor_tensor(dt_split[:, 1, :, :], ps_misc[:, :].rearrange("p (k t) -> p k t", k=KC),
                                        dt_split[:, 0, :, :].bitcast(F32), ALU.subtract).then_inc(dt_lo, 1)

            def scale_and_bias(tile, s):
                dve.wait_ge(xres_in, 16 * SUBS * (tile + 1))
                dve.wait_ge(ffn_scaled, SUBS * (tile + 1))
                dve.wait_ge(ffn_done, SUBS * tile + s + 1)
                nc.vector.scalar_tensor_tensor(out_rows[:, s, :], ps_misc[:, :], ascale[:, s:s + 1], bias[:, :],
                                               ALU.mult, ALU.add).then_inc(ffn_biased, 1)

            def run_tile(tile, first):
                dve.wait_ge(x_hi, tile + 1)
                nc.vector.tensor_tensor(xs[:, 1, :, :], x_raw[:, :, :], xs[:, 0, :, :].bitcast(F32), ALU.subtract
                                        ).then_inc(x_lo, 1)
                if first:
                    dve.wait_ge(const_in, 64)
                else:
                    block_scales(tile - 1, 0)
                split_lo_b(tile, 0)
                if first:
                    split_lo_weights(0)
                dve.wait_ge(t_done, tile + 1)
                nc.vector.tensor_tensor(t_psum, t_psum,
                                        block_mask[:, :].unsqueeze(1).to_broadcast([P, 2, TILE]), ALU.mult
                                        ).then_inc(t_masked, 1)
                if not first:
                    block_scales(tile - 1, 1)
                dve.wait_ge(t_hi, tile + 1)
                nc.vector.tensor_tensor(t_split[:, 1, :, :], t_psum, t_split[:, 0, :, :].bitcast(F32),
                                        ALU.subtract).then_inc(t_lo, 1)
                split_ad(tile, 0)
                for f in range(FC):
                    w = WIDTHS[f]
                    if f + 1 < FC:
                        split_lo_b(tile, f + 1)
                        split_ad(tile, f + 1)
                        if first:
                            split_lo_weights(f + 1)
                    dve.wait_ge(silu_done, FC * tile + f + 1)
                    dve.wait_ge(up_done, FC * tile + f + 1)
                    nc.vector.tensor_tensor(act_full[0:w, f % 2, :], ps_up[0:w, f % 2, 0:TILE],
                                            act_full[0:w, f % 2, :], ALU.mult).then_inc(act_done, 1)
                    dve.wait_ge(act_hi, FC * tile + f + 1)
                    nc.vector.tensor_tensor(act_split[0:w, 1, f % 2, :], act_full[0:w, f % 2, :],
                                            act_split[0:w, 0, f % 2, :].bitcast(F32), ALU.subtract
                                            ).then_inc(act_lo, 1)
                    if not first and f in (0, 2):
                        split_lo_transposed(tile - 1, f // 2)
                    if not first and f in (1, 3):
                        scale_and_bias(tile - 1, f // 2)
                if first:
                    for k in range(KC):
                        convert_wq(k)
                dve.wait_ge(td_done, FC * (tile + 1))
                nc.vector.tensor_tensor(td_psum, td_psum, block_mask[:, :], ALU.mult
                                        ).then_inc(td_masked, 1)
                dve.wait_ge(td_masked, tile + 1)
                nc.vector.tensor_copy(td_split[:, 0, :], td_psum).then_inc(td_hi, 1)
                dve.wait_ge(td_hi, tile + 1)
                nc.vector.tensor_tensor(td_split[:, 1, :], td_psum, td_split[:, 0, :].bitcast(F32),
                                        ALU.subtract).then_inc(td_ready, 1)

            run_tile(0, True)
            with dve.Fori(1, TILES) as tile:
                run_tile(tile, False)
            for s in range(SUBS):
                block_scales(TILES - 1, s)
            for s in range(SUBS):
                split_lo_transposed(TILES - 1, s)
                scale_and_bias(TILES - 1, s)

        @block.tensor
        def _(pe):
            HI, LO = 0, 1
            PASSES = [(HI, HI), (LO, HI), (HI, LO)]

            def lora_a(tile):
                pe.wait_ge(a_ready, tile + 1)
                pe.wait_ge(x_hi, tile + 1)
                for g in range(2):
                    for n, (ws, xp) in enumerate(PASSES):
                        if g == 0 and xp == LO:
                            pe.wait_ge(x_lo, tile + 1)
                        for k in range(KC):
                            last = nc.tensor.matmul(ps_misc[:, g * TILE:(g + 1) * TILE],
                                                    a_split[:, ws, k, g, :, :], xs[:, xp, k, :],
                                                    start=(n == 0 and k == 0), stop=(n == 2 and k == KC - 1))
                last.then_inc(t_done, 1)

            def project_main(ps_out, f, g):
                w = WIDTHS[f]
                for n, (ws, xp) in enumerate(PASSES):
                    for k in range(KC):
                        nc.tensor.matmul(ps_out[0:w, f % 2, 0:TILE], wgu_chunk(ws, f)[:, k, g, :], xs[:, xp, k, :],
                                         start=(n == 0 and k == 0), stop=False)

            def project_lora(ps_out, f, g, done):
                w = WIDTHS[f]
                for n, (ws, tp) in enumerate(PASSES):
                    last = nc.tensor.matmul(ps_out[0:w, f % 2, 0:TILE], b_split[:, ws, f % 2, g, 0:w],
                                            t_split[:, tp, g, :], start=False, stop=(n == 2))
                last.then_inc(done, 1)

            def gate_and_up(tile, f, first):
                if f >= 2:
                    pe.wait_ge(act_done, FC * tile + f - 1)
                elif not first:
                    pe.wait_ge(act_done, FC * tile - f)
                if first:
                    pe.wait_ge(wgu_lo, f + 1)
                project_main(ps_gate, f, 0)
                if f == 0:
                    project_main(ps_up, f, 1)
                    pe.wait_ge(t_lo, tile + 1)
                pe.wait_ge(b_lo, FC * tile + f + 1)
                project_lora(ps_gate, f, 0, gate_done)
                if f > 0:
                    project_main(ps_up, f, 1)
                project_lora(ps_up, f, 1, up_done)

            def lora_a_down(tile, f):
                w = WIDTHS[f]
                pe.wait_ge(ad_ready, FC * tile + f + 1)
                pe.wait_ge(act_lo, FC * tile + f + 1)
                for n, (ws, ap) in enumerate(PASSES):
                    last = nc.tensor.matmul(ps_td[:, 0:TILE], ad_split[0:w, ws, f % 2, :, :],
                                            act_split[0:w, ap, f % 2, :],
                                            start=(f == 0 and n == 0), stop=(f == FC - 1 and n == 2))
                last.then_inc(td_done, 1)

            def down(tile, f, first):
                w = WIDTHS[f]
                if first:
                    pe.wait_ge(wd_lo, f + 1)
                elif f == 0:
                    pe.wait_ge(norm_ready, SUBS * tile)
                for s in range(SUBS):
                    for n, (ap, wp) in enumerate(PASSES):
                        last = nc.tensor.matmul(ps_down[:, s, :], act_split[0:w, ap, f % 2, s * P:(s + 1) * P],
                                                wd[0:w, wp, f, :], start=(f == 0 and n == 0), stop=False)
                last.then_inc(down_done, 1)

            def lora_b_down(tile):
                pe.wait_ge(bd_ready, tile + 1)
                pe.wait_ge(td_ready, tile + 1)
                for s in range(SUBS):
                    for n, (tp, bp) in enumerate(PASSES):
                        last = nc.tensor.matmul(ps_down[:, s, :], td_split[:, tp, s * P:(s + 1) * P],
                                                bd_split[:, bp, :], start=False, stop=(n == 2))
                    last.then_inc(blocks_done, 1)

            def transpose_block(tile, s, in_tile):
                pe.wait_ge(norm_ready, SUBS * tile + s + 1)
                if s > 0:
                    pe.wait_ge(ffn_biased, SUBS * tile + s)
                elif in_tile:
                    pe.wait_ge(t_lo, tile + 2)
                for k in range(KC):
                    last = nc.tensor.transpose(ps_misc[:, k * P:(k + 1) * P], norm[:, s, k * P:(k + 1) * P],
                                               identity[:, :])
                last.then_inc(transposed, 1)

            def ffn_block(tile, s):
                pe.wait_ge(dt_lo, SUBS * tile + s + 1)
                pe.wait_ge(wq_ready, KC)
                for part in (HI, LO):
                    for k in range(KC):
                        last = nc.tensor.matmul(ps_misc[:, :], dt_split[:, part, k, :], wq[:, k, :],
                                                start=(part == HI and k == 0), stop=(part == LO and k == KC - 1))
                last.then_inc(ffn_done, 1)

            def run_tile(tile, first):
                lora_a(tile)
                for f in range(FC):
                    gate_and_up(tile, f, first)
                    if f > 0:
                        lora_a_down(tile, f - 1)
                        down(tile, f - 1, first)
                    if not first and f in (0, 2):
                        transpose_block(tile - 1, f // 2, True)
                    if not first and f in (1, 3):
                        ffn_block(tile - 1, f // 2)
                lora_a_down(tile, FC - 1)
                down(tile, FC - 1, first)
                lora_b_down(tile)

            run_tile(0, True)
            with pe.Fori(1, TILES) as tile:
                run_tile(tile, False)
            for s in range(SUBS):
                transpose_block(TILES - 1, s, False)
                ffn_block(TILES - 1, s)


def kernel(x, itok_B_2_6, L0_cond_W_gate, L0_cond_W_up, L0_cond_W_down, L0_cond_A_gate, L0_cond_B_gate,
           L0_cond_A_up, L0_cond_B_up, L0_cond_A_down, L0_cond_B_down, L0_ffn_weight_2bit, L0_ffn_weight_scale,
           L0_ffn_bias):
    import concourse.bacc as bacc
    from concourse.bass_utils import run_bass_kernel_spmd

    a = np.asarray
    x_tok = a(x).reshape(TOKENS, H)
    x_feat = x_tok.reshape(TILES, TILE, KC, P).transpose(0, 3, 2, 1)

    def by_chunk(gate, up):
        return [np.stack([gate[..., f * P:f * P + w], up[..., f * P:f * P + w]], axis=-2)
                for f, w in enumerate(WIDTHS)]

    wt = [a(w).T.reshape(KC, P, FF).transpose(1, 0, 2) for w in (L0_cond_W_gate, L0_cond_W_up)]
    w_gu = np.concatenate([c.reshape(P, -1) for c in by_chunk(*wt)], axis=1)
    w_down = a(L0_cond_W_down).T
    w_2bit = a(L0_ffn_weight_2bit).T.reshape(KC, P, H).transpose(1, 0, 2)
    a_gu = np.stack([a(m)[0].reshape(LORAS, RANK, KC, P).transpose(0, 3, 2, 1)
                     for m in (L0_cond_A_gate, L0_cond_A_up)], axis=3).reshape(LORAS, P, AGU)
    ad = np.zeros((LORAS, RANK, FC * P), a(L0_cond_A_down).dtype)
    ad[:, :, :FF] = a(L0_cond_A_down)[0]
    a_down = ad.reshape(LORAS, RANK, FC, P).transpose(0, 3, 2, 1).reshape(LORAS, P, FC * RANK)
    bt = [a(m)[0].transpose(0, 2, 1) for m in (L0_cond_B_gate, L0_cond_B_up, L0_cond_B_down)]
    b_rows = np.concatenate([c.reshape(LORAS, RANK, -1) for c in by_chunk(bt[0], bt[1])] + [bt[2]], axis=2)
    scale_col = np.broadcast_to(a(L0_ffn_weight_scale).reshape(1, 1), (P, 1))
    bias_rows = np.broadcast_to(a(L0_ffn_bias).reshape(1, H), (P, H))
    entry_of_row = np.arange(P)[:, None] // RANK
    entry_of_token = np.arange(TILE)[None, :] // SEQ
    block_mask = np.where(entry_of_row == entry_of_token, SCALE, 0.0).astype(np.float32)
    identity = np.eye(P, dtype=np.float32)
    index = a(itok_B_2_6).reshape(1, -1)

    nc = bacc.Bacc("TRN2", target_bir_lowering=False, num_devices=1, dynamic_dma_scratch_size=1024)
    arrays, args = {}, []
    for name, v in [("x_tok", x_tok), ("x_feat", x_feat), ("lora_index", index), ("w_gu", w_gu),
                    ("w_down", w_down), ("w_2bit", w_2bit), ("a_gu", a_gu), ("a_down", a_down),
                    ("b_rows", b_rows), ("scale_col", scale_col), ("bias_rows", bias_rows),
                    ("block_mask_in", block_mask), ("identity_in", identity)]:
        v = np.ascontiguousarray(v)
        arrays[name] = v
        args.append(nc.dram_tensor(name, v.shape, mybir.dt.from_np(v.dtype), kind="ExternalInput").ap())
    args.append(nc.dram_tensor("out", (TOKENS, H), F32, kind="ExternalOutput").ap())
    build(nc, *args)
    result = run_bass_kernel_spmd(nc, [arrays], core_ids=[0])
    return result.results[0]["out"].reshape(x.shape)
```

```python
from contextlib import ExitStack

import numpy as np

import concourse.bass as bass
from concourse import mybir

F32 = mybir.dt.float32
F32R = mybir.dt.float32r
I32 = mybir.dt.int32
ALU = mybir.AluOpType
ACT = mybir.ActivationFunctionType
AX_X = mybir.AxisListType.X

P = 128
TOKENS = 4096
SEQ = 32
TILE = 256
TILES = TOKENS // TILE
BATCH = TOKENS // SEQ
ENTRIES = TILE // SEQ
SUBS = TILE // P
H = 512
KC = H // P
FF = 1376
WIDTHS = [min(P, FF - f * P) for f in range(-(-FF // P))]
FC = len(WIDTHS)
RANK = 16
LORAS = 16
SCALE = 0.5
PAIR = 2 * RANK
STACK = 3 * PAIR
EPS = 1e-5
AGU = 2 * KC * RANK
FIRST = 6
ROW = 2 * FF + H
PIECES = [(0, FIRST), (FIRST, FC)]


def piece_columns(piece):
    a, b = PIECES[piece]
    return 2 * a * P, 2 * min(b * P, FF)


PLAN_COLUMNS_STEP = 8
WQ_FROM = FC - KC


def wd_turn(f):
    return f + max(0, f - WQ_FROM)


def wq_turn(k):
    return WQ_FROM + 2 * k + 1


def build(nc, x_tok, x_feat, lora_index, places, pair_masks, w_gu, w_down, w_2bit, a_gu, a_down, b_rows, scale_col, bias_rows,
          block_mask_in, identity_in, out):
    with ExitStack() as ctx:
        def sb(name, shape, dt=F32):
            return ctx.enter_context(nc.sbuf_tensor(name, shape, dt))

        def ps(name, shape):
            return ctx.enter_context(nc.psum_tensor(name, shape, F32))

        def sem(name):
            return ctx.enter_context(nc.semaphore(name))

        wgu = sb("wgu", [P, 2, 2 * FF * KC], F32R)
        wd = sb("wd", [P, 2, FC, H], F32R)
        wq = sb("wq", [P, KC, H], F32R)
        x_raw = sb("x_raw", [P, ENTRIES, KC * SEQ])
        xs = sb("xs", [P, 2, KC, TILE], F32R)
        a_raw = sb("a_raw", [P, ENTRIES, AGU])
        a_split = sb("a_split", [P, 2, KC, 2 * ENTRIES * RANK], F32R)
        b_raw = sb("b_raw", [P, 2 * FF])
        b_split = sb("b_split", [P, 2, 2, 2, P], F32R)
        ad_raw = sb("ad_raw", [P, ENTRIES, FC * RANK])
        ad_split = sb("ad_split", [P, 2, 2 * ENTRIES * RANK], F32R)
        bd_raw = sb("bd_raw", [P, H])
        bd_split = sb("bd_split", [P, 2, H], F32R)
        t_split = sb("t_split", [P, 2, 2, TILE], F32R)
        td_split = sb("td_split", [P, 2, TILE], F32R)
        act_full = sb("act_full", [P, 2, TILE])
        act_split = sb("act_split", [P, 2, 2, TILE], F32R)
        rows = sb("rows", [P, 3 * SUBS, H])
        norm = rows[:, 0:SUBS, :]
        x_res = rows[:, SUBS:2 * SUBS, :]
        out_rows = rows[:, 2 * SUBS:3 * SUBS, :]
        dt_split = sb("dt_split", [P, 2, KC, P], F32R)
        bias = sb("bias", [P, H])
        block_mask = sb("block_mask", [P, TILE])
        mask_gu = block_mask[0:2 * PAIR, :]
        mask_d = block_mask[2 * PAIR:3 * PAIR, :]
        td_lo_part = block_mask[3 * PAIR:4 * PAIR, :]
        identity = sb("identity", [P, P])
        wscale = sb("wscale", [P, 1])
        amax = sb("amax", [P, SUBS])
        ones = sb("ones", [P, 1])
        rinv = sb("rinv", [P, SUBS])
        ascale = sb("ascale", [P, SUBS])
        plan = sb("plan", [P, BATCH], I32)
        stage_gu = rows[:, 0:4, :].rearrange("p (s a) h -> p s (a h)", s=2)
        stage_d = rows[:, 4:6, :]

        ps_down = ps("ps_down", [P, SUBS, 512])
        ps_td = ps("ps_td", [P, 512])
        ps_gate = ps("ps_gate", [P, 2, 512])
        ps_up = ps("ps_up", [P, 2, 512])
        ps_misc = ps("ps_misc", [P, 512])
        ps_last = [ps_misc[:, :], ps_gate[:, 0, :]]
        t_psum = ps_misc[:, :].rearrange("p (g t) -> p g t", g=2)
        td_psum = ps_td[:, 0:TILE]

        index_in = sem("index_in")
        plan_cleared = sem("plan_cleared")
        plan_steps = sem("plan_steps")
        plan_gathered = sem("plan_gathered")
        plan_ready = sem("plan_ready")
        mask_gu_in = sem("mask_gu_in")
        mask_d_in = sem("mask_d_in")
        t_hi_again = sem("t_hi_again")
        td_copied = sem("td_copied")
        td_summed = sem("td_summed")
        td_hi_again = sem("td_hi_again")
        ones_ready = sem("ones_ready")
        table_ready = sem("table_ready")
        const_in = sem("const_in")
        mask_in = sem("mask_in")
        x_in = sem("x_in")
        a_in = sem("a_in")
        b_in = [sem(f"b{n}_in") for n in range(2)]
        ad_in = [sem(f"ad{n}_in") for n in range(2)]
        bd_in = sem("bd_in")
        xres_in = sem("xres_in")
        wgu_in = [sem(f"wgu{n}_in") for n in range(2)]
        wd_in = [sem(f"wd{n}_in") for n in range(2)]
        stored = sem("stored")
        wgu_hi = sem("wgu_hi")
        wgu_lo = sem("wgu_lo")
        wd_hi = sem("wd_hi")
        wd_lo = sem("wd_lo")
        wq_ready = sem("wq_ready")
        x_hi = sem("x_hi")
        x_lo = sem("x_lo")
        a_hi = sem("a_hi")
        a_ready = sem("a_ready")
        b_hi = sem("b_hi")
        b_lo = sem("b_lo")
        ad_hi = sem("ad_hi")
        ad_ready = sem("ad_ready")
        bd_hi = sem("bd_hi")
        bd_ready = sem("bd_ready")
        t_masked = sem("t_masked")
        t_hi = sem("t_hi")
        t_lo = sem("t_lo")
        td_masked = sem("td_masked")
        td_hi = sem("td_hi")
        td_ready = sem("td_ready")
        silu_done = sem("silu_done")
        act_done = sem("act_done")
        act_hi = sem("act_hi")
        act_lo = sem("act_lo")
        amax_steps = sem("amax_steps")
        ascale_ready = sem("ascale_ready")
        norm_ready = sem("norm_ready")
        dt_hi = sem("dt_hi")
        dt_lo = sem("dt_lo")
        ffn_biased = sem("ffn_biased")
        ffn_scaled = sem("ffn_scaled")
        out_ready = sem("out_ready")
        t_done = sem("t_done")
        gate_done = sem("gate_done")
        up_done = sem("up_done")
        td_done = sem("td_done")
        down_done = sem("down_done")
        blocks_done = sem("blocks_done")
        transposed = sem("transposed")
        ffn_done = sem("ffn_done")

        def scratch(at, n):
            return b_raw[:, at:at + n]

        idx_places = scratch(0, BATCH + 1).bitcast(I32)
        number_places = scratch(256, BATCH + 1)
        keys = scratch(512, BATCH + 1)
        compared = scratch(768, BATCH)
        one_hot = scratch(896, BATCH)
        plan_columns = scratch(1024, 96)
        rank_col = scratch(1152, 1)
        run_key = scratch(1153, 1)
        tile_rows = scratch(1160, TILES)
        most_changes = scratch(1180, 1)[32:33, :]
        sorted_idx = scratch(1280, BATCH)[32:33, :]
        changes = scratch(1408, TILES * (ENTRIES - 1))[32:33, :].rearrange("p (t e) -> p t e", t=TILES)
        ps_plan = ps_misc[0:96, 0:BATCH]

        def chunk_gu(f):
            return f * P * 2 * KC, 2 * KC * WIDTHS[f]

        def a_raw_chunk(k, n):
            return a_raw[:, 0:n, k * 2 * RANK:(k + 1) * 2 * RANK].rearrange("p e (g r) -> p g e r", g=2)

        def a_split_chunk(part, k, n):
            return a_split[:, part, k, 0:2 * n * RANK].rearrange("p (g e r) -> p g e r", g=2, e=n)

        def ad_split_chunk(part, slot, n):
            return ad_split[:, slot, part * n * RANK:(part + 1) * n * RANK]

        def loras(pair):
            return 2 if pair else ENTRIES

        def b_piece_dmas(pair):
            return 4 if pair else ENTRIES

        x_by_chunk = x_raw[:, :, :].rearrange("p e (k t) -> p k e t", k=KC)

        def xs_split(part):
            return xs[:, part, :, :].rearrange("p k (e t) -> p k e t", e=ENTRIES)

        def pair_flag(eng):
            eng.wait_ge(plan_ready, 1)
            return eng.value_load(plan[3 * 32:3 * 32 + 1, TILES:TILES + 1], min_val=0, max_val=1)

        def wgu_chunk(part, f):
            at, n = chunk_gu(f)
            return wgu[:, part, at:at + n].rearrange("p (k g w) -> p k g w", k=KC, g=2)

        block = ctx.enter_context(nc.Block())

        @block.sync
        def _(sp):
            def entry_at(tile, e):
                return sp.value_load(plan[0:1, bass.ds(tile * ENTRIES + e, 1)], min_val=0, max_val=BATCH - 1)

            def lora_at(tile, e):
                return sp.value_load(plan[32:33, bass.ds(tile * ENTRIES + e, 1)], min_val=0, max_val=LORAS - 1)

            def load_x(tile):
                if not (isinstance(tile, int) and tile == 0):
                    sp.wait_ge(x_lo, tile)
                for e in range(ENTRIES):
                    sp.dma_start(x_raw[:, e, :], x_feat[bass.ds(entry_at(tile, e), 1), :, :]
                                 .rearrange("a p n -> (a p) n")).then_inc(x_in, 16)

            def tile_loras(tile, pair):
                return [lora_at(tile, e) for e in ((0, ENTRIES - 1) if pair else range(ENTRIES))]

            def gather_a(idx):
                for e in range(len(idx)):
                    sp.dma_start(a_raw[:, e, :], a_gu[bass.ds(idx[e], 1), :, :].rearrange("a p n -> (a p) n")
                                 ).then_inc(a_in, 16)

            def gather_rows(dst, idx, a, b, done):
                for copy in range(2 if len(idx) == 2 else 1):
                    for e in range(len(idx)):
                        at = copy * PAIR + e * RANK
                        sp.dma_start(dst[at:at + RANK, :], b_rows[bass.ds(idx[e], 1), :, a:b]
                                     .rearrange("a r n -> (a r) n")).then_inc(done, 16)

            def gather_b(idx, piece):
                a, b = piece_columns(piece)
                gather_rows(b_raw[:, a:b], idx, a, b, b_in[piece])

            def gather_ad(idx, piece):
                f0, f1 = PIECES[piece]
                for e in range(len(idx)):
                    sp.dma_start(ad_raw[:, e, f0 * RANK:f1 * RANK],
                                 a_down[bass.ds(idx[e], 1), :, f0 * RANK:f1 * RANK].rearrange("a p n -> (a p) n")
                                 ).then_inc(ad_in[piece], 16)

            def gather_bd(idx):
                gather_rows(bd_raw, idx, 2 * FF, ROW, bd_in)

            def first_run(tile):
                return sp.value_load(plan[96:97, bass.ds(tile, 1)], min_val=0, max_val=ENTRIES)

            def load_mask_gu(tile):
                if not (isinstance(tile, int) and tile == 0):
                    sp.wait_ge(t_masked, tile)
                sp.dma_start(mask_gu, pair_masks[bass.ds(first_run(tile), 1), :, :].rearrange("a p n -> (a p) n")
                             ).then_inc(mask_gu_in, 16)

            def load_mask_d(tile):
                if not (isinstance(tile, int) and tile == 0):
                    sp.wait_ge(td_masked, tile)
                sp.dma_start(mask_d, pair_masks[bass.ds(first_run(tile), 1), 0:PAIR, :]
                             .rearrange("a p n -> (a p) n")).then_inc(mask_d_in, 16)

            def rows_used(tile, piece):
                sp.wait_ge(b_lo, FC * (tile - 1) + PIECES[piece][1])
                sp.wait_ge(ad_ready, FC * (tile - 1) + PIECES[piece][1])

            def load_residual(tile):
                for e in range(ENTRIES):
                    s, at = e * SEQ // P, e * SEQ % P
                    sp.dma_start(x_res[at:at + SEQ, s, :], x_tok[bass.ds(entry_at(tile, e), 1), :, :]
                                 .rearrange("a t n -> (a t) n")).then_inc(xres_in, 16)

            def load_wgu(f):
                at, n = chunk_gu(f)
                sp.wait_ge(wgu_lo, f - 1)
                sp.dma_start(stage_gu[:, f % 2, 0:n], w_gu[:, at:at + n]).then_inc(wgu_in[f % 2], 16)

            def load_wd(f):
                n = wd_turn(f)
                if f >= 2:
                    sp.wait_ge(wd_lo, f - 1 if f <= WQ_FROM else f)
                sp.dma_start(stage_d[0:WIDTHS[f], n % 2, :], w_down[f * P:f * P + WIDTHS[f], :]
                             ).then_inc(wd_in[n % 2], 16)

            def load_wq(k):
                n = wq_turn(k)
                if k == 0:
                    sp.wait_ge(wd_lo, WQ_FROM)
                else:
                    sp.wait_ge(wq_ready, k)
                sp.dma_start(stage_d[:, n % 2, :].bitcast(I32), w_2bit[:, k, :]).then_inc(wd_in[n % 2], 16)

            def store(tile):
                for s in range(SUBS):
                    sp.wait_ge(out_ready, SUBS * tile + s + 1)
                    for at in range(0, P, SEQ):
                        entry = entry_at(tile, (s * P + at) // SEQ)
                        sp.dma_start(out[bass.ds(entry, 1), :, :].rearrange("a t n -> (a t) n"),
                                     out_rows[at:at + SEQ, s, :]).then_inc(stored, 16)

            def whole_program(pair):
                load_x(0)
                idx = tile_loras(0, pair)
                gather_a(idx)
                if pair:
                    load_mask_gu(0)
                else:
                    sp.dma_start(block_mask[:, :], block_mask_in).then_inc(mask_in, 16)
                gather_b(idx, 0)
                load_wgu(2)
                load_wd(0)
                gather_ad(idx, 0)
                load_wd(1)
                sp.dma_start(identity[:, :], identity_in).then_inc(const_in, 16)
                sp.dma_start(wscale[:, :], scale_col).then_inc(const_in, 16)
                sp.dma_start(bias[:, :], bias_rows).then_inc(const_in, 16)
                load_wgu(3)
                load_wd(2)
                gather_b(idx, 1)
                load_wgu(4)
                load_wd(3)
                gather_ad(idx, 1)
                load_wgu(5)
                load_wd(4)
                gather_bd(idx)
                load_wgu(6)
                load_wd(5)
                load_wgu(7)
                load_wd(6)
                load_x(1)
                idx = tile_loras(1, pair)
                sp.wait_ge(a_ready, 1)
                gather_a(idx)
                if pair:
                    load_mask_gu(1)
                    load_mask_d(0)
                load_wgu(8)
                load_wd(7)
                load_wq(0)
                rows_used(1, 0)
                gather_b(idx, 0)
                load_wgu(9)
                load_wd(8)
                load_wq(1)
                gather_ad(idx, 0)
                load_wgu(10)
                for k in (2, 3):
                    load_wd(WQ_FROM + k)
                    load_wq(k)
                rows_used(1, 1)
                gather_b(idx, 1)
                gather_ad(idx, 1)
                sp.wait_ge(bd_ready, 1)
                gather_bd(idx)
                sp.wait_ge(wq_ready, KC)
                load_residual(0)

                with sp.Fori(2, TILES) as tile:
                    idx = tile_loras(tile, pair)
                    load_x(tile)
                    sp.wait_ge(a_ready, tile)
                    gather_a(idx)
                    if pair:
                        load_mask_gu(tile)
                        load_mask_d(tile - 1)
                    rows_used(tile, 0)
                    gather_b(idx, 0)
                    gather_ad(idx, 0)
                    store(tile - 2)
                    rows_used(tile, 1)
                    gather_b(idx, 1)
                    gather_ad(idx, 1)
                    sp.wait_ge(bd_ready, tile)
                    gather_bd(idx)
                    sp.wait_ge(stored, 16 * ENTRIES * (tile - 1))
                    load_residual(tile - 1)
                if pair:
                    load_mask_d(TILES - 1)
                store(TILES - 2)
                sp.wait_ge(stored, 16 * ENTRIES * (TILES - 1))
                load_residual(TILES - 1)
                store(TILES - 1)
                sp.wait_ge(stored, 16 * ENTRIES * TILES)

            sp.dma_start(idx_places, lora_index).then_inc(index_in, 16)
            sp.dma_start(number_places, places).then_inc(index_in, 16)
            flag = pair_flag(sp)
            with sp.If(flag == 1):
                whole_program(True)
            with sp.Else():
                whole_program(False)

        @block.gpsimd
        def _(pool):
            def split_a(tile, pair):
                n = loras(pair)
                pool.wait_ge(t_done, tile)
                pool.wait_ge(a_in, 16 * n * (tile + 1))
                for k in range(KC):
                    pool.tensor_tensor(a_split_chunk(0, k, n), a_raw_chunk(k, n),
                                       ones[:, :, None, None].to_broadcast([P, 2, n, RANK]), ALU.mult
                                       ).then_inc(a_hi, 1)
                for k in range(KC):
                    pool.wait_ge(a_hi, KC * tile + k + 1)
                    last = pool.tensor_tensor(a_split_chunk(1, k, n), a_raw_chunk(k, n),
                                              a_split_chunk(0, k, n).bitcast(F32), ALU.subtract)
                last.then_inc(a_ready, 1)

            def split_bd(tile, pair):
                if not (isinstance(tile, int) and tile == 0):
                    pool.wait_ge(blocks_done, SUBS * tile)
                pool.wait_ge(bd_in, 16 * b_piece_dmas(pair) * (tile + 1))
                rows_hi = 2 * PAIR if pair else P
                pool.tensor_tensor(bd_split[0:rows_hi, 0, :], bd_raw[0:rows_hi, :],
                                   ones[0:rows_hi, :].to_broadcast([rows_hi, H]), ALU.mult).then_inc(bd_hi, 1)
                pool.wait_ge(bd_hi, tile + 1)
                rows_in = PAIR if pair else P
                lo = bd_split[2 * PAIR:STACK, 0, :] if pair else bd_split[:, 1, :]
                pool.tensor_tensor(lo, bd_raw[0:rows_in, :], bd_split[0:rows_in, 0, :].bitcast(F32),
                                   ALU.subtract).then_inc(bd_ready, 1)
                if pair:
                    pool.wait_ge(bd_ready, tile + 1)

            def add_residual(tile):
                pool.wait_ge(xres_in, 16 * ENTRIES * (tile + 1))
                for s in range(SUBS):
                    pool.wait_ge(ffn_biased, SUBS * tile + s + 1)
                    pool.tensor_tensor(out_rows[:, s, :], x_res[:, s, :], out_rows[:, s, :], ALU.add
                                       ).then_inc(out_ready, 1)

            def whole_program(pair):
                split_bd(0, pair)
                split_a(1, pair)
                with pool.Fori(1, TILES - 1) as tile:
                    split_bd(tile, pair)
                    add_residual(tile - 1)
                    split_a(tile + 1, pair)
                split_bd(TILES - 1, pair)
                add_residual(TILES - 2)

            pool.memset(ones[:, :], 1.0).then_inc(ones_ready, 1)
            pool.memset(plan_columns, 0.0).then_inc(plan_cleared, 1)
            pool.wait_ge(ones_ready, 1)
            flag = pair_flag(pool)
            with pool.If(flag == 1):
                whole_program(True)
            with pool.Else():
                whole_program(False)

        @block.scalar
        def _(act):
            def split_hi_wgu(f):
                at, n = chunk_gu(f)
                act.wait_ge(wgu_in[f % 2], 16 * (f // 2 + 1))
                nc.scalar.activation(wgu[:, 0, at:at + n], stage_gu[:, f % 2, 0:n], ACT.Copy).then_inc(wgu_hi, 1)

            def split_hi_wd(f):
                w, n = WIDTHS[f], wd_turn(f)
                act.wait_ge(wd_in[n % 2], 16 * (n // 2 + 1))
                nc.scalar.activation(wd[0:w, 0, f, :], stage_d[0:w, n % 2, :], ACT.Copy).then_inc(wd_hi, 1)

            def split_hi_b(tile, f, pair):
                w = WIDTHS[f]
                at = 2 * P * f
                n = 2 * PAIR if pair else P
                act.wait_ge(b_in[f >= FIRST], 16 * b_piece_dmas(pair) * (tile + 1))
                if f >= 2:
                    act.wait_ge(up_done, FC * tile + f - 1)
                elif not (isinstance(tile, int) and tile == 0):
                    act.wait_ge(up_done, FC * tile - f)
                nc.scalar.activation(b_split[0:n, 0, f % 2, :, 0:w],
                                     b_raw[0:n, at:at + 2 * w].rearrange("p (g w) -> p g w", g=2), ACT.Copy
                                     ).then_inc(b_hi, 1)

            def normalise(tile, s):
                act.wait_ge(ascale_ready, SUBS * tile + s + 1)
                nc.scalar.activation(norm[:, s, :], ps_down[:, s, :], ACT.Copy, scale=rinv[:, s:s + 1]
                                     ).then_inc(norm_ready, 1)

            def split_hi_transposed(tile, s, ps_block):
                act.wait_ge(transposed, SUBS * tile + s + 1)
                if s > 0 or not (isinstance(tile, int) and tile == 0):
                    act.wait_ge(ffn_done, SUBS * tile + s)
                nc.scalar.activation(dt_split[:, 0, :, :], ps_block.rearrange("p (k t) -> p k t", k=KC),
                                     ACT.Copy).then_inc(dt_hi, 1)

            def split_hi_t(tile, pair):
                act.wait_ge(t_masked, tile + 1)
                if not pair:
                    nc.scalar.activation(t_split[:, 0, :, :], t_psum, ACT.Copy).then_inc(t_hi, 1)
                    return
                for g in range(2):
                    last = nc.scalar.activation(t_split[0:PAIR, 0, g, :], ps_misc[g * PAIR:(g + 1) * PAIR, 0:TILE],
                                                ACT.Copy)
                last.then_inc(t_hi, 1)
                act.wait_ge(t_hi, tile + 1)
                nc.scalar.activation(t_split[2 * PAIR:STACK, 0, :, :], t_split[0:PAIR, 0, :, :].bitcast(F32), ACT.Copy
                                     ).then_inc(t_hi_again, 1)

            def copy_down_lora(tile):
                act.wait_ge(td_done, FC * (tile + 1))
                nc.scalar.activation(td_lo_part, ps_td[PAIR:2 * PAIR, 0:TILE], ACT.Copy).then_inc(td_copied, 1)

            def split_hi_down_lora(tile):
                act.wait_ge(td_masked, tile + 1)
                nc.scalar.activation(td_split[0:PAIR, 0, :], ps_td[0:PAIR, 0:TILE], ACT.Copy).then_inc(td_hi, 1)
                act.wait_ge(td_hi, tile + 1)
                nc.scalar.activation(td_split[2 * PAIR:STACK, 0, :], td_split[0:PAIR, 0, :].bitcast(F32), ACT.Copy
                                     ).then_inc(td_hi_again, 1)

            def run_tile(tile, first, pair):
                act.wait_ge(x_in, 16 * ENTRIES * (tile + 1))
                if not first:
                    act.wait_ge(up_done, FC * tile)
                nc.scalar.activation(xs_split(0), x_by_chunk, ACT.Copy).then_inc(x_hi, 1)
                if first:
                    act.wait_ge(a_in, 16 * loras(pair))
                    for k in range(KC):
                        nc.scalar.activation(a_split_chunk(0, k, loras(pair)), a_raw_chunk(k, loras(pair)),
                                             ACT.Copy).then_inc(a_hi, 1)
                elif pair:
                    copy_down_lora(tile - 1)
                    split_hi_down_lora(tile - 1)
                split_hi_b(tile, 0, pair)
                split_hi_t(tile, pair)
                if first:
                    split_hi_wd(0)
                else:
                    for s in range(SUBS):
                        normalise(tile - 1, s)
                for f in range(FC):
                    w = WIDTHS[f]
                    if f + 1 < FC:
                        split_hi_b(tile, f + 1, pair)
                        if first:
                            split_hi_wd(f + 1)
                    if first and f + 2 < FC:
                        split_hi_wgu(f + 2)
                    act.wait_ge(gate_done, FC * tile + f + 1)
                    if f >= 2:
                        act.wait_ge(act_lo, FC * tile + f - 1)
                    elif not first:
                        act.wait_ge(act_lo, FC * tile - f)
                    nc.scalar.activation(act_full[0:w, f % 2, :], ps_gate[0:w, f % 2, 0:TILE], ACT.Silu
                                         ).then_inc(silu_done, 1)
                    act.wait_ge(act_done, FC * tile + f + 1)
                    nc.scalar.activation(act_split[0:w, 0, f % 2, :], act_full[0:w, f % 2, :], ACT.Copy
                                         ).then_inc(act_hi, 1)
                    if not first and f in (0, 2):
                        split_hi_transposed(tile - 1, f // 2, ps_misc[:, :])

            act.wait_ge(ones_ready, 1)
            nc.scalar.activation(rinv[:, 0:1], ones[:, :], ACT.Silu).then_inc(table_ready, 1)
            for f in range(2):
                at, n = chunk_gu(f)
                act.dma_start(stage_gu[:, f, 0:n], w_gu[:, at:at + n]).then_inc(wgu_in[f], 16)
            split_hi_wgu(0)
            split_hi_wgu(1)

            def whole_program(pair):
                run_tile(0, True, pair)
                with act.Fori(1, TILES) as tile:
                    run_tile(tile, False, pair)
                if pair:
                    copy_down_lora(TILES - 1)
                    split_hi_down_lora(TILES - 1)
                for s in range(SUBS):
                    normalise(TILES - 1, s)
                for s in range(SUBS):
                    split_hi_transposed(TILES - 1, s, ps_last[s])

            flag = pair_flag(act)
            with act.If(flag == 1):
                whole_program(True)
            with act.Else():
                whole_program(False)

        @block.vector
        def _(dve):
            def split_lo_wgu(f):
                at, n = chunk_gu(f)
                dve.wait_ge(wgu_hi, f + 1)
                nc.vector.tensor_tensor(wgu[:, 1, at:at + n], stage_gu[:, f % 2, 0:n],
                                        wgu[:, 0, at:at + n].bitcast(F32), ALU.subtract).then_inc(wgu_lo, 1)

            def split_lo_wd(f):
                w, n = WIDTHS[f], wd_turn(f)
                dve.wait_ge(wd_hi, f + 1)
                nc.vector.tensor_tensor(wd[0:w, 1, f, :], stage_d[0:w, n % 2, :], wd[0:w, 0, f, :].bitcast(F32),
                                        ALU.subtract).then_inc(wd_lo, 1)

            def convert_wq(k):
                n = wq_turn(k)
                dve.wait_ge(wd_in[n % 2], 16 * (n // 2 + 1))
                nc.vector.tensor_scalar(wq[:, k, :], stage_d[:, n % 2, :].bitcast(I32), -1.5, None, ALU.add
                                        ).then_inc(wq_ready, 1)

            def split_lo_b(tile, f, pair):
                w = WIDTHS[f]
                at = 2 * P * f
                n = PAIR if pair else P
                lo = b_split[2 * PAIR:STACK, 0, f % 2, :, 0:w] if pair else b_split[:, 1, f % 2, :, 0:w]
                dve.wait_ge(b_hi, FC * tile + f + 1)
                nc.vector.tensor_tensor(lo, b_raw[0:n, at:at + 2 * w].rearrange("p (g w) -> p g w", g=2),
                                        b_split[0:n, 0, f % 2, :, 0:w].bitcast(F32), ALU.subtract
                                        ).then_inc(b_lo, 1)

            def split_ad(tile, f, pair):
                n = loras(pair)
                dve.wait_ge(ad_in[f >= FIRST], 16 * n * (tile + 1))
                if f >= 2:
                    dve.wait_ge(td_done, FC * tile + f - 1)
                elif not (isinstance(tile, int) and tile == 0):
                    dve.wait_ge(td_done, FC * tile - f)
                raw = ad_raw[:, 0:n, f * RANK:(f + 1) * RANK]
                hi, lo = (ad_split_chunk(part, f % 2, n).rearrange("p (e r) -> p e r", e=n) for part in range(2))
                nc.vector.tensor_copy(hi, raw).then_inc(ad_hi, 1)
                dve.wait_ge(ad_hi, FC * tile + f + 1)
                nc.vector.tensor_tensor(lo, raw, hi.bitcast(F32), ALU.subtract).then_inc(ad_ready, 1)

            def block_scales(tile, s):
                done = 2 * (SUBS * tile + s)
                dve.wait_ge(blocks_done, SUBS * tile + s + 1)
                nc.vector.tensor_reduce(amax[:, s:s + 1], ps_down[:, s, :], AX_X, ALU.max,
                                        apply_absolute_value=True).then_inc(amax_steps, 1)
                dve.wait_ge(amax_steps, done + 1)
                nc.vector.tensor_scalar(amax[:, s:s + 1], amax[:, s:s + 1], EPS, None, ALU.max
                                        ).then_inc(amax_steps, 1)
                dve.wait_ge(amax_steps, done + 2)
                nc.vector.tensor_tensor(ascale[:, s:s + 1], amax[:, s:s + 1], wscale[:, :], ALU.mult
                                        ).then_inc(ffn_scaled, 1)
                nc.vector.reciprocal(rinv[:, s:s + 1], amax[:, s:s + 1]).then_inc(ascale_ready, 1)

            def split_lo_transposed(tile, s, ps_block):
                dve.wait_ge(dt_hi, SUBS * tile + s + 1)
                nc.vector.tensor_tensor(dt_split[:, 1, :, :], ps_block.rearrange("p (k t) -> p k t", k=KC),
                                        dt_split[:, 0, :, :].bitcast(F32), ALU.subtract).then_inc(dt_lo, 1)

            def mask_t(tile, pair):
                dve.wait_ge(t_done, tile + 1)
                if pair:
                    dve.wait_ge(mask_gu_in, 16 * (tile + 1))
                    t_rows = ps_misc[0:2 * PAIR, 0:TILE]
                    nc.vector.tensor_tensor(t_rows, t_rows, mask_gu, ALU.mult).then_inc(t_masked, 1)
                else:
                    nc.vector.tensor_tensor(t_psum, t_psum, block_mask[:, :].unsqueeze(1).to_broadcast([P, 2, TILE]),
                                            ALU.mult).then_inc(t_masked, 1)

            def split_lo_t(tile, pair):
                dve.wait_ge(t_hi, tile + 1)
                if pair:
                    for g in range(2):
                        last = nc.vector.tensor_tensor(t_split[PAIR:2 * PAIR, 0, g, :],
                                                       ps_misc[g * PAIR:(g + 1) * PAIR, 0:TILE],
                                                       t_split[0:PAIR, 0, g, :].bitcast(F32), ALU.subtract)
                    last.then_inc(t_lo, 1)
                else:
                    nc.vector.tensor_tensor(t_split[:, 1, :, :], t_psum, t_split[:, 0, :, :].bitcast(F32),
                                            ALU.subtract).then_inc(t_lo, 1)

            def split_down_lora(tile, pair):
                if pair:
                    sums = ps_td[0:PAIR, 0:TILE]
                    dve.wait_ge(td_copied, tile + 1)
                    nc.vector.tensor_tensor(sums, sums, td_lo_part, ALU.add).then_inc(td_summed, 1)
                    dve.wait_ge(td_summed, tile + 1)
                    dve.wait_ge(mask_d_in, 16 * (tile + 1))
                    nc.vector.tensor_tensor(sums, sums, mask_d, ALU.mult).then_inc(td_masked, 1)
                    dve.wait_ge(td_hi, tile + 1)
                    nc.vector.tensor_tensor(td_split[PAIR:2 * PAIR, 0, :], sums, td_split[0:PAIR, 0, :].bitcast(F32),
                                            ALU.subtract).then_inc(td_ready, 1)
                    return
                dve.wait_ge(td_done, FC * (tile + 1))
                nc.vector.tensor_tensor(td_psum, td_psum, block_mask[:, :], ALU.mult).then_inc(td_masked, 1)
                dve.wait_ge(td_masked, tile + 1)
                nc.vector.tensor_copy(td_split[:, 0, :], td_psum).then_inc(td_hi, 1)
                dve.wait_ge(td_hi, tile + 1)
                nc.vector.tensor_tensor(td_split[:, 1, :], td_psum, td_split[:, 0, :].bitcast(F32),
                                        ALU.subtract).then_inc(td_ready, 1)

            def scale_and_bias(tile, s, ps_block):
                dve.wait_ge(xres_in, 16 * ENTRIES * (tile + 1))
                dve.wait_ge(ffn_scaled, SUBS * (tile + 1))
                dve.wait_ge(ffn_done, SUBS * tile + s + 1)
                nc.vector.scalar_tensor_tensor(out_rows[:, s, :], ps_block, ascale[:, s:s + 1], bias[:, :],
                                               ALU.mult, ALU.add).then_inc(ffn_biased, 1)

            def run_tile(tile, first, pair):
                dve.wait_ge(x_hi, tile + 1)
                nc.vector.tensor_tensor(xs_split(1), x_by_chunk, xs_split(0).bitcast(F32), ALU.subtract
                                        ).then_inc(x_lo, 1)
                if first:
                    for k in range(KC):
                        dve.wait_ge(a_hi, k + 1)
                        last = nc.vector.tensor_tensor(a_split_chunk(1, k, loras(pair)),
                                                       a_raw_chunk(k, loras(pair)),
                                                       a_split_chunk(0, k, loras(pair)).bitcast(F32),
                                                       ALU.subtract)
                    last.then_inc(a_ready, 1)
                    if not pair:
                        dve.wait_ge(mask_in, 16)
                else:
                    split_down_lora(tile - 1, pair)
                split_lo_b(tile, 0, pair)
                mask_t(tile, pair)
                split_lo_t(tile, pair)
                if first:
                    split_lo_wd(0)
                else:
                    for s in range(SUBS):
                        block_scales(tile - 1, s)
                split_ad(tile, 0, pair)
                for f in range(FC):
                    w = WIDTHS[f]
                    if f + 1 < FC:
                        split_lo_b(tile, f + 1, pair)
                        if first:
                            split_lo_wd(f + 1)
                            if f + 1 >= WQ_FROM:
                                convert_wq(f + 1 - WQ_FROM)
                    if first and f + 2 < FC:
                        split_lo_wgu(f + 2)
                    dve.wait_ge(silu_done, FC * tile + f + 1)
                    dve.wait_ge(up_done, FC * tile + f + 1)
                    nc.vector.tensor_tensor(act_full[0:w, f % 2, :], ps_up[0:w, f % 2, 0:TILE],
                                            act_full[0:w, f % 2, :], ALU.mult).then_inc(act_done, 1)
                    dve.wait_ge(act_hi, FC * tile + f + 1)
                    nc.vector.tensor_tensor(act_split[0:w, 1, f % 2, :], act_full[0:w, f % 2, :],
                                            act_split[0:w, 0, f % 2, :].bitcast(F32), ALU.subtract
                                            ).then_inc(act_lo, 1)
                    if f + 1 < FC:
                        split_ad(tile, f + 1, pair)
                    if not first and f in (0, 2):
                        split_lo_transposed(tile - 1, f // 2, ps_misc[:, :])
                    if not first and f in (1, 3):
                        scale_and_bias(tile - 1, f // 2, ps_misc[:, :])
                if first:
                    dve.wait_ge(const_in, 48)

            def make_plan():
                step = [0]

                def then(instruction):
                    instruction.then_inc(plan_steps, 1)
                    step[0] += 1
                    dve.wait_ge(plan_steps, step[0])

                tt, ts, red = nc.vector.tensor_tensor, nc.vector.tensor_scalar, nc.vector.tensor_reduce
                dve.wait_ge(index_in, 32)
                dve.wait_ge(plan_cleared, 1)
                then(nc.vector.scalar_tensor_tensor(keys, idx_places, float(BATCH), number_places, ALU.mult, ALU.add))
                then(ts(compared, keys[:, 0:BATCH], keys[:, BATCH:BATCH + 1], None, ALU.is_lt))
                then(red(rank_col, compared, AX_X, ALU.add))
                then(ts(one_hot, number_places[:, 0:BATCH], rank_col, None, ALU.is_equal))
                then(ts(run_key, idx_places[:, BATCH:BATCH + 1], float(BATCH), BATCH - 0.5, ALU.mult, ALU.add))
                then(ts(compared, keys[:, 0:BATCH], run_key, None, ALU.is_lt))
                then(red(plan_columns[:, 64:65], compared, AX_X, ALU.add))
                nc.vector.tensor_copy(plan_columns[:, 32:33], idx_places[:, BATCH:BATCH + 1])
                then(nc.vector.tensor_copy(plan_columns[:, 0:1], number_places[:, BATCH:BATCH + 1]))
                dve.wait_ge(plan_gathered, 1)
                nc.vector.tensor_copy(plan[0:96, :], ps_plan)
                then(nc.vector.tensor_copy(sorted_idx, ps_plan[32:33, :]))
                then(tt(tile_rows[64:65, :], ps_plan[64:65, 0:BATCH:ENTRIES],
                        number_places[64:65, 0:BATCH:ENTRIES], ALU.subtract))
                ts(plan[96:97, 0:TILES], tile_rows[64:65, :], float(ENTRIES), None, ALU.min)
                now = ps_plan[32:33, :].rearrange("p (t e) -> p t e", e=ENTRIES)[:, :, 0:ENTRIES - 1]
                following = sorted_idx.rearrange("p (t e) -> p t e", e=ENTRIES)[:, :, 1:ENTRIES]
                then(tt(changes, now, following, ALU.not_equal))
                then(red(tile_rows[32:33, :], changes, AX_X, ALU.add))
                then(red(most_changes, tile_rows[32:33, :], AX_X, ALU.max))
                ts(plan[96:97, TILES:TILES + 1], most_changes, 1.0, None, ALU.is_le).then_inc(plan_ready, 1)

            def whole_program(pair):
                run_tile(0, True, pair)
                with dve.Fori(1, TILES) as tile:
                    run_tile(tile, False, pair)
                split_down_lora(TILES - 1, pair)
                for s in range(SUBS):
                    block_scales(TILES - 1, s)
                split_lo_transposed(TILES - 1, 0, ps_last[0])
                scale_and_bias(TILES - 1, 0, ps_last[0])
                split_lo_transposed(TILES - 1, 1, ps_last[1])
                dve.wait_ge(ffn_biased, SUBS * TILES - 1)
                nc.vector.tensor_tensor(out_rows[:, 0, :], x_res[:, 0, :], out_rows[:, 0, :], ALU.add
                                        ).then_inc(out_ready, 1)
                scale_and_bias(TILES - 1, 1, ps_last[1])
                dve.wait_ge(ffn_biased, SUBS * TILES)
                nc.vector.tensor_tensor(out_rows[:, 1, :], x_res[:, 1, :], out_rows[:, 1, :], ALU.add
                                        ).then_inc(out_ready, 1)

            make_plan()
            split_lo_wgu(0)
            split_lo_wgu(1)
            flag = pair_flag(dve)
            with dve.If(flag == 1):
                whole_program(True)
            with dve.Else():
                whole_program(False)

        @block.tensor
        def _(pe):
            HI, LO = 0, 1
            PASSES = [(HI, HI), (LO, HI), (HI, LO)]

            def lora_a(tile, pair):
                pe.wait_ge(a_ready, tile + 1)
                pe.wait_ge(x_hi, tile + 1)
                for g in range(1 if pair else 2):
                    for n, (ws, xp) in enumerate(PASSES):
                        if g == 0 and xp == LO:
                            pe.wait_ge(x_lo, tile + 1)
                        for k in range(KC):
                            a = a_split[:, ws, k, 0:2 * PAIR] if pair else a_split[:, ws, k, g * P:(g + 1) * P]
                            last = nc.tensor.matmul(ps_misc[0:2 * PAIR if pair else P, g * TILE:(g + 1) * TILE],
                                                    a, xs[:, xp, k, :],
                                                    start=(n == 0 and k == 0), stop=(n == 2 and k == KC - 1))
                last.then_inc(t_done, 1)

            def main_pass(ps_out, f, g, ws, xp, start=False):
                for k in range(KC):
                    nc.tensor.matmul(ps_out[0:WIDTHS[f], f % 2, 0:TILE], wgu_chunk(ws, f)[:, k, g, :],
                                     xs[:, xp, k, :], start=(start and k == 0), stop=False)

            def project_main(ps_out, f, g):
                for n, (ws, xp) in enumerate(PASSES):
                    main_pass(ps_out, f, g, ws, xp, n == 0)

            def first_products():
                pe.wait_ge(x_hi, 1)
                pe.wait_ge(wgu_hi, 1)
                main_pass(ps_gate, 0, 0, HI, HI, True)
                main_pass(ps_up, 0, 1, HI, HI, True)
                pe.wait_ge(x_lo, 1)
                main_pass(ps_gate, 0, 0, HI, LO)
                main_pass(ps_up, 0, 1, HI, LO)
                pe.wait_ge(wgu_lo, 1)
                main_pass(ps_gate, 0, 0, LO, HI)
                main_pass(ps_up, 0, 1, LO, HI)

            def project_lora(ps_out, f, g, done, pair):
                w = WIDTHS[f]
                if pair:
                    last = nc.tensor.matmul(ps_out[0:w, f % 2, 0:TILE], b_split[0:STACK, 0, f % 2, g, 0:w],
                                            t_split[0:STACK, 0, g, :], start=False, stop=True)
                else:
                    for n, (ws, tp) in enumerate(PASSES):
                        last = nc.tensor.matmul(ps_out[0:w, f % 2, 0:TILE], b_split[:, ws, f % 2, g, 0:w],
                                                t_split[:, tp, g, :], start=False, stop=(n == 2))
                last.then_inc(done, 1)

            def main_products(tile, f, first):
                slots_free(tile, f, first)
                project_main(ps_gate, f, 0)
                project_main(ps_up, f, 1)

            def slots_free(tile, f, first):
                if f >= 2:
                    pe.wait_ge(act_done, FC * tile + f - 1)
                elif not first:
                    pe.wait_ge(act_done, FC * tile - f)
                if first:
                    pe.wait_ge(wgu_lo, f + 1)

            def gate_and_up(tile, f, first, pair):
                slots_free(tile, f, first)
                project_main(ps_gate, f, 0)
                pe.wait_ge(b_lo, FC * tile + f + 1)
                project_lora(ps_gate, f, 0, gate_done, pair)
                project_main(ps_up, f, 1)
                project_lora(ps_up, f, 1, up_done, pair)

            def add_lora(tile, f, pair):
                pe.wait_ge(t_lo, tile + 1)
                if pair:
                    pe.wait_ge(t_hi_again, tile + 1)
                pe.wait_ge(b_lo, FC * tile + f + 1)
                project_lora(ps_gate, f, 0, gate_done, pair)
                project_lora(ps_up, f, 1, up_done, pair)

            def lora_a_down(tile, f, pair):
                w = WIDTHS[f]
                pe.wait_ge(ad_ready, FC * tile + f + 1)
                pe.wait_ge(act_lo, FC * tile + f + 1)
                if pair:
                    for part in ((HI, LO) if f == 0 else (LO, HI)):
                        m = 2 * PAIR if part == HI else PAIR
                        last = nc.tensor.matmul(ps_td[0:m, 0:TILE], ad_split[0:w, f % 2, 0:m],
                                                act_split[0:w, part, f % 2, :], start=(f == 0 and part == HI),
                                                stop=(f == FC - 1 and part == HI))
                else:
                    for n, (ws, ap) in enumerate(PASSES):
                        last = nc.tensor.matmul(ps_td[:, 0:TILE], ad_split[0:w, f % 2, ws * P:(ws + 1) * P],
                                                act_split[0:w, ap, f % 2, :],
                                                start=(f == 0 and n == 0), stop=(f == FC - 1 and n == 2))
                last.then_inc(td_done, 1)

            def down(tile, f, first):
                w = WIDTHS[f]
                if first:
                    pe.wait_ge(wd_lo, f + 1)
                elif f == 0:
                    pe.wait_ge(norm_ready, SUBS * tile)
                for s in range(SUBS):
                    for n, (ap, wp) in enumerate(PASSES):
                        last = nc.tensor.matmul(ps_down[:, s, :], act_split[0:w, ap, f % 2, s * P:(s + 1) * P],
                                                wd[0:w, wp, f, :], start=(f == 0 and n == 0), stop=False)
                last.then_inc(down_done, 1)

            def lora_b_down(tile, pair):
                pe.wait_ge(bd_ready, tile + 1)
                pe.wait_ge(td_ready, tile + 1)
                if pair:
                    pe.wait_ge(td_hi_again, tile + 1)
                for s in range(SUBS):
                    if pair:
                        last = nc.tensor.matmul(ps_down[:, s, :], td_split[0:STACK, 0, s * P:(s + 1) * P],
                                                bd_split[0:STACK, 0, :], start=False, stop=True)
                    else:
                        for n, (tp, bp) in enumerate(PASSES):
                            last = nc.tensor.matmul(ps_down[:, s, :], td_split[:, tp, s * P:(s + 1) * P],
                                                    bd_split[:, bp, :], start=False, stop=(n == 2))
                    last.then_inc(blocks_done, 1)

            def transpose_block(tile, s, ps_block):
                pe.wait_ge(norm_ready, SUBS * tile + s + 1)
                for k in range(KC):
                    last = nc.tensor.transpose(ps_block[:, k * P:(k + 1) * P], norm[:, s, k * P:(k + 1) * P],
                                               identity[:, :])
                last.then_inc(transposed, 1)

            def ffn_block(tile, s, ps_block):
                pe.wait_ge(wq_ready, KC)
                pe.wait_ge(dt_lo, SUBS * tile + s + 1)
                for part in (HI, LO):
                    for k in range(KC):
                        last = nc.tensor.matmul(ps_block, dt_split[:, part, k, :], wq[:, k, :],
                                                start=(part == HI and k == 0), stop=(part == LO and k == KC - 1))
                last.then_inc(ffn_done, 1)

            def run_tile(tile, first, pair):
                if first:
                    first_products()
                    main_products(0, 1, True)
                    lora_a(0, pair)
                    add_lora(0, 0, pair)
                else:
                    lora_a(tile, pair)
                    lora_b_down(tile - 1, pair)
                    main_products(tile, 0, False)
                    add_lora(tile, 0, pair)
                for f in range(FC):
                    if f == 1 and first:
                        add_lora(0, 1, pair)
                    elif f > 0:
                        gate_and_up(tile, f, first, pair)
                    if f > 0:
                        lora_a_down(tile, f - 1, pair)
                        down(tile, f - 1, first)
                    if not first and f in (0, 2):
                        if f == 0:
                            pe.wait_ge(t_lo, tile + 1)
                        else:
                            pe.wait_ge(ffn_biased, SUBS * tile - 1)
                        transpose_block(tile - 1, f // 2, ps_misc[:, :])
                    if not first and f in (1, 3):
                        ffn_block(tile - 1, f // 2, ps_misc[:, :])
                lora_a_down(tile, FC - 1, pair)
                down(tile, FC - 1, first)

            def whole_program(pair):
                run_tile(0, True, pair)
                with pe.Fori(1, TILES) as tile:
                    run_tile(tile, False, pair)
                lora_b_down(TILES - 1, pair)
                for s in range(SUBS):
                    transpose_block(TILES - 1, s, ps_last[s])
                for s in range(SUBS):
                    ffn_block(TILES - 1, s, ps_last[s])

            pe.wait_ge(plan_steps, PLAN_COLUMNS_STEP)
            nc.tensor.matmul(ps_plan, plan_columns, one_hot, start=True, stop=True).then_inc(plan_gathered, 1)
            flag = pair_flag(pe)
            with pe.If(flag == 1):
                whole_program(True)
            with pe.Else():
                whole_program(False)


def kernel(x, itok_B_2_6, L0_cond_W_gate, L0_cond_W_up, L0_cond_W_down, L0_cond_A_gate, L0_cond_B_gate,
           L0_cond_A_up, L0_cond_B_up, L0_cond_A_down, L0_cond_B_down, L0_ffn_weight_2bit, L0_ffn_weight_scale,
           L0_ffn_bias):
    import concourse.bacc as bacc
    from concourse.bass_utils import run_bass_kernel_spmd

    a = np.asarray
    x_tok = a(x).reshape(BATCH, SEQ, H)
    x_feat = x_tok.reshape(BATCH, SEQ, KC, P).transpose(0, 3, 2, 1).reshape(BATCH, P, KC * SEQ)

    def by_chunk(gate, up):
        return [np.stack([gate[..., f * P:f * P + w], up[..., f * P:f * P + w]], axis=-2)
                for f, w in enumerate(WIDTHS)]

    wt = [a(w).T.reshape(KC, P, FF).transpose(1, 0, 2) for w in (L0_cond_W_gate, L0_cond_W_up)]
    w_gu = np.concatenate([c.reshape(P, -1) for c in by_chunk(*wt)], axis=1)
    w_down = a(L0_cond_W_down).T
    w_2bit = a(L0_ffn_weight_2bit).T.reshape(KC, P, H).transpose(1, 0, 2)
    a_gu = np.stack([a(m)[0].reshape(LORAS, RANK, KC, P).transpose(0, 3, 2, 1)
                     for m in (L0_cond_A_gate, L0_cond_A_up)], axis=3).reshape(LORAS, P, AGU)
    ad = np.zeros((LORAS, RANK, FC * P), a(L0_cond_A_down).dtype)
    ad[:, :, :FF] = a(L0_cond_A_down)[0]
    a_down = ad.reshape(LORAS, RANK, FC, P).transpose(0, 3, 2, 1).reshape(LORAS, P, FC * RANK)
    bt = [a(m)[0].transpose(0, 2, 1) for m in (L0_cond_B_gate, L0_cond_B_up, L0_cond_B_down)]
    b_rows = np.concatenate([c.reshape(LORAS, RANK, -1) for c in by_chunk(bt[0], bt[1])] + [bt[2]], axis=2)
    scale_col = np.broadcast_to(a(L0_ffn_weight_scale).reshape(1, 1), (P, 1))
    bias_rows = np.broadcast_to(a(L0_ffn_bias).reshape(1, H), (P, H))
    entry_of_row = np.arange(P)[:, None] // RANK
    entry_of_token = np.arange(TILE)[None, :] // SEQ
    block_mask = np.where(entry_of_row == entry_of_token, SCALE, 0.0).astype(np.float32)
    identity = np.eye(P, dtype=np.float32)
    index = a(itok_B_2_6).reshape(-1)
    index_rows = np.concatenate([np.broadcast_to(index, (P, BATCH)), index[:, None]], axis=1)
    number = np.arange(BATCH, dtype=np.float32)
    places = np.concatenate([np.broadcast_to(number, (P, BATCH)), number[:, None]], axis=1)
    second_row = np.arange(2 * PAIR)[None, :, None] % PAIR // RANK
    second_token = entry_of_token[None] >= np.arange(ENTRIES + 1)[:, None, None]
    pair_masks = np.where(second_row == second_token, SCALE, 0.0).astype(np.float32)

    nc = bacc.Bacc("TRN2", target_bir_lowering=False, num_devices=1, dynamic_dma_scratch_size=1024)
    arrays, args = {}, []
    for name, v in [("x_tok", x_tok), ("x_feat", x_feat), ("lora_index", index_rows),
                    ("places", places), ("pair_masks", pair_masks), ("w_gu", w_gu),
                    ("w_down", w_down), ("w_2bit", w_2bit), ("a_gu", a_gu), ("a_down", a_down),
                    ("b_rows", b_rows), ("scale_col", scale_col), ("bias_rows", bias_rows),
                    ("block_mask_in", block_mask), ("identity_in", identity)]:
        v = np.ascontiguousarray(v)
        arrays[name] = v
        args.append(nc.dram_tensor(name, v.shape, mybir.dt.from_np(v.dtype), kind="ExternalInput").ap())
    args.append(nc.dram_tensor("out", (BATCH, SEQ, H), F32, kind="ExternalOutput").ap())
    build(nc, *args)
    result = run_bass_kernel_spmd(nc, [arrays], core_ids=[0])
    return result.results[0]["out"].reshape(x.shape)
```

```python
from contextlib import ExitStack

import numpy as np

import concourse.bass as bass
from concourse import mybir

F32 = mybir.dt.float32
F32R = mybir.dt.float32r
I32 = mybir.dt.int32
ALU = mybir.AluOpType
ACT = mybir.ActivationFunctionType
AX_X = mybir.AxisListType.X

P = 128
TOKENS = 4096
SEQ = 32
TILE = 256
TILES = TOKENS // TILE
BATCH = TOKENS // SEQ
ENTRIES = TILE // SEQ
SUBS = TILE // P
H = 512
KC = H // P
FF = 1376
FC = -(-FF // P)
FIRST_WIDTH = FF - (FC - 1) * P
WIDTHS = [FIRST_WIDTH] + (FC - 1) * [P]
STARTS = [sum(WIDTHS[:f]) for f in range(FC + 1)]
RANK = 16
LORAS = 16
SCALE = 0.5
PAIR = 2 * RANK
STACK = 3 * PAIR
EPS = 1e-5
AGU = 2 * KC * RANK
FIRST = 6
ROW = 2 * FF + H
PIECES = [(0, FIRST), (FIRST, FC)]


def piece_columns(piece):
    a, b = PIECES[piece]
    return 2 * STARTS[a], 2 * STARTS[b]


PLAN_COLUMNS_STEP = 8
PLAN_ORDER_STEP = 9
WQ_FROM = FC - KC


def wd_turn(f):
    return f + max(0, f - WQ_FROM)


def wq_turn(k):
    return WQ_FROM + 2 * k + 1


def build(nc, x_tok, x_feat, lora_index, places, pair_masks, w_gu, w_down, w_2bit, a_gu, a_down, b_rows, scale_col, bias_rows,
          block_mask_in, identity_in, out):
    with ExitStack() as ctx:
        def sb(name, shape, dt=F32):
            return ctx.enter_context(nc.sbuf_tensor(name, shape, dt))

        def ps(name, shape):
            return ctx.enter_context(nc.psum_tensor(name, shape, F32))

        def sem(name):
            return ctx.enter_context(nc.semaphore(name))

        wgu = sb("wgu", [P, 2, 2 * (FF - FIRST_WIDTH) * KC], F32R)
        wgu_first = sb("wgu_first", [P, 2, KC, 2, P], F32R)
        wd = sb("wd", [P, 2, FC, H], F32R)
        wq = sb("wq", [P, KC, H], F32R)
        x_raw = sb("x_raw", [P, ENTRIES, KC * SEQ])
        xs = sb("xs", [P, 2, KC, TILE], F32R)
        a_raw = sb("a_raw", [P, ENTRIES, AGU])
        a_split = sb("a_split", [P, 2, KC, 2 * ENTRIES * RANK], F32R)
        b_raw = sb("b_raw", [P, 2 * FF])
        b_split = sb("b_split", [P, 2, 2, 2, P], F32R)
        ad_raw = sb("ad_raw", [P, ENTRIES, FC * RANK])
        ad_split = sb("ad_split", [P, 2, 2 * ENTRIES * RANK], F32R)
        bd_raw = sb("bd_raw", [P, H])
        bd_split = sb("bd_split", [P, 2, H], F32R)
        t_split = sb("t_split", [P, 2, 2, TILE], F32R)
        td_split = sb("td_split", [P, 2, TILE], F32R)
        act_full = sb("act_full", [P, 2, TILE])
        act_split = sb("act_split", [P, 2, 2, TILE], F32R)
        rows = sb("rows", [P, 3 * SUBS, H])
        norm = rows[:, 0:SUBS, :]
        x_res = rows[:, SUBS:2 * SUBS, :]
        out_rows = rows[:, 2 * SUBS:3 * SUBS, :]
        dt_split = sb("dt_split", [P, 2, KC, P], F32R)
        bias = sb("bias", [P, H])
        t_full = a_raw[0:PAIR, 2:6, :].rearrange("p a n -> p (a n)").rearrange("p (g t) -> p g t", g=2)
        td_full = a_raw[0:PAIR, 6:8, :].rearrange("p a n -> p (a n)")
        spare = ad_raw[:, 2:ENTRIES, :].rearrange("p a n -> p (a n)")
        td_lo_part = spare[0:PAIR, 0:TILE]
        mask_d = spare[0:PAIR, TILE:2 * TILE]
        mask_gu = spare[FIRST_WIDTH:P, 0:TILE]
        pair_identity = spare[:, 2 * TILE:2 * TILE + P]
        up_full = spare[0:FIRST_WIDTH, 2 * TILE + P:3 * TILE + P]
        mask_columns = wgu_first[:, 0, :, :, FIRST_WIDTH:P].rearrange("p k g c -> p (k g) c")
        identity_columns = wgu_first[:, 1, 0:2, :, FIRST_WIDTH:P].rearrange("p k g c -> p (k g) c")
        block_mask = mask_columns.bitcast(F32)
        general_identity = identity_columns.bitcast(F32)
        wscale = sb("wscale", [P, 1])
        amax = sb("amax", [P, SUBS])
        ones = sb("ones", [P, 1])
        rinv = sb("rinv", [P, SUBS])
        ascale = sb("ascale", [P, SUBS])
        plan = sb("plan", [P, BATCH // 2 + TILES + 1], I32)
        plan_run = plan[0:1, BATCH // 2:BATCH // 2 + TILES]
        plan_flag = plan[0:1, BATCH // 2 + TILES:BATCH // 2 + TILES + 1]
        stage_gu = rows[:, 0:4, :].rearrange("p (s a) h -> p s (a h)", s=2)
        stage_d = rows[:, 4:6, :]

        ps_down = ps("ps_down", [P, SUBS, 512])
        ps_td = ps("ps_td", [P, 512])
        ps_gate = ps("ps_gate", [P, 2, 512])
        ps_up = ps("ps_up", [P, 2, 512])
        ps_misc = ps("ps_misc", [P, 512])
        ps_last = [ps_misc[:, :], ps_gate[:, 0, :]]
        t_psum = ps_misc[:, :].rearrange("p (g t) -> p g t", g=2)
        td_psum = ps_td[:, 0:TILE]

        first_lora = ps_misc[0:FIRST_WIDTH, :].rearrange("p (g t) -> p g t", g=2)

        index_in = sem("index_in")
        plan_cleared = sem("plan_cleared")
        plan_steps = sem("plan_steps")
        plan_gathered = sem("plan_gathered")
        plan_ready = sem("plan_ready")
        mask_gu_in = sem("mask_gu_in")
        mask_d_in = sem("mask_d_in")
        t_hi_again = sem("t_hi_again")
        td_copied = sem("td_copied")
        td_summed = sem("td_summed")
        td_hi_again = sem("td_hi_again")
        ones_ready = sem("ones_ready")
        table_ready = sem("table_ready")
        const_in = sem("const_in")
        mask_in = sem("mask_in")
        mask_ready = sem("mask_ready")
        x_in = sem("x_in")
        first_a_in = sem("first_a_in")
        a_in = sem("a_in")
        b_in = [sem(f"b{n}_in") for n in range(2)]
        ad_in = [sem(f"ad{n}_in") for n in range(2)]
        bd_in = sem("bd_in")
        xres_in = sem("xres_in")
        wgu_in = [sem(f"wgu{n}_in") for n in range(2)]
        wd_in = [sem(f"wd{n}_in") for n in range(2)]
        stored = sem("stored")
        wgu_hi = sem("wgu_hi")
        wgu_lo = sem("wgu_lo")
        wd_hi = sem("wd_hi")
        wd_lo = sem("wd_lo")
        wq_ready = sem("wq_ready")
        x_hi = sem("x_hi")
        x_lo = sem("x_lo")
        a_hi = sem("a_hi")
        a_ready = sem("a_ready")
        b_hi = sem("b_hi")
        b_lo = sem("b_lo")
        ad_hi = sem("ad_hi")
        ad_ready = sem("ad_ready")
        bd_hi = sem("bd_hi")
        bd_ready = sem("bd_ready")
        t_masked = sem("t_masked")
        t_hi = sem("t_hi")
        t_lo = sem("t_lo")
        td_masked = sem("td_masked")
        td_hi = sem("td_hi")
        td_ready = sem("td_ready")
        gate_copied = sem("gate_copied")
        up_copied = sem("up_copied")
        gate_summed = sem("gate_summed")
        up_summed = sem("up_summed")
        silu_done = sem("silu_done")
        act_done = sem("act_done")
        act_hi = sem("act_hi")
        act_lo = sem("act_lo")
        amax_steps = sem("amax_steps")
        ascale_ready = sem("ascale_ready")
        norm_ready = sem("norm_ready")
        dt_hi = sem("dt_hi")
        dt_lo = sem("dt_lo")
        ffn_biased = sem("ffn_biased")
        ffn_scaled = sem("ffn_scaled")
        out_ready = sem("out_ready")
        t_done = sem("t_done")
        gate_done = sem("gate_done")
        up_done = sem("up_done")
        td_done = sem("td_done")
        down_done = sem("down_done")
        blocks_done = sem("blocks_done")
        transposed = sem("transposed")
        ffn_done = sem("ffn_done")

        def scratch(at, n):
            return b_raw[:, at:at + n]

        idx_places = scratch(0, BATCH + 1).bitcast(I32)
        number_places = scratch(256, BATCH + 1)
        keys = scratch(512, BATCH + 1)
        compared = scratch(768, BATCH)
        one_hot = scratch(896, BATCH)
        plan_columns = scratch(1024, 96)
        rank_col = scratch(1152, 1)
        run_key = scratch(1153, 1)
        tile_rows = scratch(1160, TILES)
        most_changes = scratch(1180, 1)[32:33, :]
        sorted_idx = scratch(1280, BATCH)[32:33, :]
        changes = scratch(1408, TILES * (ENTRIES - 1))[32:33, :].rearrange("p (t e) -> p t e", t=TILES)
        ps_plan = ps_misc[0:96, 0:BATCH]

        def chunk_gu(f):
            return STARTS[f] * 2 * KC, 2 * KC * WIDTHS[f]

        def a_raw_chunk(k, n):
            return a_raw[:, 0:n, k * 2 * RANK:(k + 1) * 2 * RANK].rearrange("p e (g r) -> p g e r", g=2)

        def a_split_chunk(part, k, n):
            if n == 2:
                return wgu_first[:, part, k, :, FIRST_WIDTH:P].rearrange("p g (e r) -> p g e r", e=n)
            return a_split[:, part, k, 0:2 * n * RANK].rearrange("p (g e r) -> p g e r", g=2, e=n)

        def ad_split_chunk(part, slot, n):
            return ad_split[:, slot, part * n * RANK:(part + 1) * n * RANK]

        def loras(pair):
            return 2 if pair else ENTRIES

        def b_piece_dmas(pair):
            return 4 if pair else ENTRIES

        x_by_chunk = x_raw[:, :, :].rearrange("p e (k t) -> p k e t", k=KC)

        def xs_split(part):
            return xs[:, part, :, :].rearrange("p k (e t) -> p k e t", e=ENTRIES)

        def plan_at(first_row, tile, e):
            half, at = divmod(e, ENTRIES // 2)
            row = first_row + 32 * half
            return plan[row:row + 1, bass.ds(tile * (ENTRIES // 2) + at, 1)]

        def entry_at(eng, tile, e):
            return eng.value_load(plan_at(0, tile, e), min_val=0, max_val=BATCH - 1)

        def lora_at(eng, tile, e):
            return eng.value_load(plan_at(64, tile, e), min_val=0, max_val=LORAS - 1)

        def load_x_entry(eng, tile, e):
            eng.dma_start(x_raw[:, e, :], x_feat[bass.ds(entry_at(eng, tile, e), 1), :, :]
                          .rearrange("a p n -> (a p) n")).then_inc(x_in, 16)

        def load_a(eng, idx, e, done):
            eng.dma_start(a_raw[:, e, :], a_gu[bass.ds(idx, 1), :, :].rearrange("a p n -> (a p) n")).then_inc(done, 16)

        def a_loads(tile, pair):
            return 16 * loras(pair) * (tile if pair else tile + 1)

        def load_wgu(eng, f):
            at, n = chunk_gu(f)
            if f >= 2:
                eng.wait_ge(wgu_lo, f - 1)
            eng.dma_start(stage_gu[:, f % 2, 0:n], w_gu[:, at:at + n]).then_inc(wgu_in[f % 2], 16)

        def load_wd(eng, f):
            n = wd_turn(f)
            if f >= 2:
                eng.wait_ge(wd_lo, f - 1 if f <= WQ_FROM else f)
            eng.dma_start(stage_d[0:WIDTHS[f], n % 2, :], w_down[STARTS[f]:STARTS[f + 1], :]
                          ).then_inc(wd_in[n % 2], 16)

        def pair_flag(eng):
            eng.wait_ge(plan_ready, 1)
            return eng.value_load(plan_flag, min_val=0, max_val=1)

        def wgu_chunk(part, f):
            if f == 0:
                return wgu_first[:, part, :, :, 0:FIRST_WIDTH]
            at, n = chunk_gu(f)
            at -= chunk_gu(1)[0]
            return wgu[:, part, at:at + n].rearrange("p (k g w) -> p k g w", k=KC, g=2)

        def stage_gu_chunk(f):
            return stage_gu[:, f % 2, 0:chunk_gu(f)[1]].rearrange("p (k g w) -> p k g w", k=KC, g=2)

        block = ctx.enter_context(nc.Block())

        @block.sync
        def _(sp):
            def load_x(tile, first_entry=0, end=ENTRIES):
                sp.wait_ge(x_lo, tile)
                for e in range(first_entry, end):
                    load_x_entry(sp, tile, e)

            def tile_loras(tile, pair):
                return [lora_at(sp, tile, e) for e in ((0, ENTRIES - 1) if pair else range(ENTRIES))]

            def gather_a(idx):
                for e in range(len(idx)):
                    load_a(sp, idx[e], e, a_in)

            def gather_rows(dst, idx, a, b, done):
                for copy in range(2 if len(idx) == 2 else 1):
                    for e in range(len(idx)):
                        at = copy * PAIR + e * RANK
                        sp.dma_start(dst[at:at + RANK, :], b_rows[bass.ds(idx[e], 1), :, a:b]
                                     .rearrange("a r n -> (a r) n")).then_inc(done, 16)

            def gather_b(idx, piece):
                a, b = piece_columns(piece)
                gather_rows(b_raw[:, a:b], idx, a, b, b_in[piece])

            def gather_ad(idx, piece):
                f0, f1 = PIECES[piece]
                for e in range(len(idx)):
                    sp.dma_start(ad_raw[:, e, f0 * RANK:f1 * RANK],
                                 a_down[bass.ds(idx[e], 1), :, f0 * RANK:f1 * RANK].rearrange("a p n -> (a p) n")
                                 ).then_inc(ad_in[piece], 16)

            def gather_bd(idx):
                gather_rows(bd_raw, idx, 2 * FF, ROW, bd_in)

            def first_run(tile):
                return sp.value_load(plan_run[:, bass.ds(tile, 1)], min_val=0, max_val=ENTRIES)

            def load_mask_gu(tile):
                if not (isinstance(tile, int) and tile == 0):
                    sp.wait_ge(t_masked, tile)
                sp.dma_start(mask_gu, pair_masks[bass.ds(first_run(tile), 1), :, :].rearrange("a p n -> (a p) n")
                             ).then_inc(mask_gu_in, 16)

            def load_mask_d(tile):
                if not (isinstance(tile, int) and tile == 0):
                    sp.wait_ge(td_masked, tile)
                sp.dma_start(mask_d, pair_masks[bass.ds(first_run(tile), 1), :, :]
                             .rearrange("a p n -> (a p) n")).then_inc(mask_d_in, 16)

            def rows_used(tile, piece):
                sp.wait_ge(b_lo, FC * (tile - 1) + PIECES[piece][1])
                sp.wait_ge(ad_ready, FC * (tile - 1) + PIECES[piece][1])

            def load_residual(tile):
                for e in range(ENTRIES):
                    s, at = e * SEQ // P, e * SEQ % P
                    sp.dma_start(x_res[at:at + SEQ, s, :], x_tok[bass.ds(entry_at(sp, tile, e), 1), :, :]
                                 .rearrange("a t n -> (a t) n")).then_inc(xres_in, 16)

            def load_wq(k):
                n = wq_turn(k)
                if k == 0:
                    sp.wait_ge(wd_lo, WQ_FROM)
                else:
                    sp.wait_ge(wq_ready, k)
                sp.dma_start(stage_d[:, n % 2, :].bitcast(I32), w_2bit[:, k, :]).then_inc(wd_in[n % 2], 16)

            def store(tile):
                for s in range(SUBS):
                    sp.wait_ge(out_ready, SUBS * tile + s + 1)
                    for at in range(0, P, SEQ):
                        entry = entry_at(sp, tile, (s * P + at) // SEQ)
                        sp.dma_start(out[bass.ds(entry, 1), :, :].rearrange("a t n -> (a t) n"),
                                     out_rows[at:at + SEQ, s, :]).then_inc(stored, 16)

            def whole_program(pair):
                idx = tile_loras(0, pair)
                if not pair:
                    sp.wait_ge(first_a_in, 32)
                    gather_a(idx)
                if pair:
                    load_mask_gu(0)
                else:
                    sp.dma_start(bd_raw[:, 0:TILE], block_mask_in).then_inc(mask_in, 16)
                    sp.dma_start(bd_raw[:, TILE:TILE + P], identity_in).then_inc(mask_in, 16)
                gather_b(idx, 0)
                gather_ad(idx, 0)
                if pair:
                    sp.dma_start(pair_identity, identity_in).then_inc(const_in, 16)
                sp.dma_start(wscale[:, :], scale_col).then_inc(const_in, 16)
                sp.dma_start(bias[:, :], bias_rows).then_inc(const_in, 16)
                load_wgu(sp, 3)
                load_wd(sp, 2)
                gather_b(idx, 1)
                load_wgu(sp, 4)
                load_wd(sp, 3)
                gather_ad(idx, 1)
                load_x(1, 0, 2)
                load_wgu(sp, 5)
                load_wd(sp, 4)
                if not pair:
                    sp.wait_ge(mask_ready, 2)
                gather_bd(idx)
                load_wgu(sp, 6)
                load_wd(sp, 5)
                load_x(1, 2, 5)
                load_wgu(sp, 7)
                load_wd(sp, 6)
                load_x(1, 5, ENTRIES)
                idx = tile_loras(1, pair)
                load_wgu(sp, 8)
                load_wd(sp, 7)
                load_wq(0)
                sp.wait_ge(a_ready, 1)
                gather_a(idx)
                if pair:
                    load_mask_gu(1)
                    load_mask_d(0)
                rows_used(1, 0)
                gather_b(idx, 0)
                load_wgu(sp, 9)
                load_wd(sp, 8)
                load_wq(1)
                gather_ad(idx, 0)
                load_wgu(sp, 10)
                for k in (2, 3):
                    load_wd(sp, WQ_FROM + k)
                    load_wq(k)
                rows_used(1, 1)
                gather_b(idx, 1)
                gather_ad(idx, 1)
                sp.wait_ge(bd_ready, 1)
                gather_bd(idx)
                sp.wait_ge(wq_ready, KC)
                load_residual(0)

                with sp.Fori(2, TILES) as tile:
                    idx = tile_loras(tile, pair)
                    load_x(tile)
                    sp.wait_ge(a_ready, tile)
                    gather_a(idx)
                    if pair:
                        load_mask_gu(tile)
                        load_mask_d(tile - 1)
                    rows_used(tile, 0)
                    gather_b(idx, 0)
                    gather_ad(idx, 0)
                    store(tile - 2)
                    rows_used(tile, 1)
                    gather_b(idx, 1)
                    gather_ad(idx, 1)
                    sp.wait_ge(bd_ready, tile)
                    gather_bd(idx)
                    sp.wait_ge(stored, 16 * ENTRIES * (tile - 1))
                    load_residual(tile - 1)
                if pair:
                    load_mask_d(TILES - 1)
                store(TILES - 2)
                sp.wait_ge(stored, 16 * ENTRIES * (TILES - 1))
                load_residual(TILES - 1)
                store(TILES - 1)
                sp.wait_ge(stored, 16 * ENTRIES * TILES)

            sp.dma_start(idx_places, lora_index).then_inc(index_in, 16)
            sp.dma_start(number_places, places).then_inc(index_in, 16)
            sp.wait_ge(plan_steps, PLAN_ORDER_STEP)
            for e in range(0, ENTRIES, 2):
                load_x_entry(sp, 0, e)
            load_a(sp, lora_at(sp, 0, 0), 0, first_a_in)
            flag = pair_flag(sp)
            with sp.If(flag == 1):
                whole_program(True)
            with sp.Else():
                whole_program(False)

        @block.gpsimd
        def _(pool):
            def split_a(tile, pair):
                n = loras(pair)
                pool.wait_ge(t_done, tile)
                pool.wait_ge(a_in, a_loads(tile, pair))
                for k in range(KC):
                    pool.tensor_tensor(a_split_chunk(0, k, n), a_raw_chunk(k, n),
                                       ones[:, :, None, None].to_broadcast([P, 2, n, RANK]), ALU.mult
                                       ).then_inc(a_hi, 1)
                for k in range(KC):
                    pool.wait_ge(a_hi, KC * tile + k + 1)
                    last = pool.tensor_tensor(a_split_chunk(1, k, n), a_raw_chunk(k, n),
                                              a_split_chunk(0, k, n).bitcast(F32), ALU.subtract)
                last.then_inc(a_ready, 1)

            def split_bd(tile, pair):
                if not (isinstance(tile, int) and tile == 0):
                    pool.wait_ge(blocks_done, SUBS * tile)
                pool.wait_ge(bd_in, 16 * b_piece_dmas(pair) * (tile + 1))
                rows_hi = 2 * PAIR if pair else P
                pool.tensor_tensor(bd_split[0:rows_hi, 0, :], bd_raw[0:rows_hi, :],
                                   ones[0:rows_hi, :].to_broadcast([rows_hi, H]), ALU.mult).then_inc(bd_hi, 1)
                pool.wait_ge(bd_hi, tile + 1)
                rows_in = PAIR if pair else P
                lo = bd_split[2 * PAIR:STACK, 0, :] if pair else bd_split[:, 1, :]
                pool.tensor_tensor(lo, bd_raw[0:rows_in, :], bd_split[0:rows_in, 0, :].bitcast(F32),
                                   ALU.subtract).then_inc(bd_ready, 1)
                if pair:
                    pool.wait_ge(bd_ready, tile + 1)

            def add_residual(tile):
                pool.wait_ge(xres_in, 16 * ENTRIES * (tile + 1))
                for s in range(SUBS):
                    pool.wait_ge(ffn_biased, SUBS * tile + s + 1)
                    pool.tensor_tensor(out_rows[:, s, :], x_res[:, s, :], out_rows[:, s, :], ALU.add
                                       ).then_inc(out_ready, 1)

            def place_mask_and_identity():
                pool.wait_ge(mask_in, 32)
                for columns, at in ((mask_columns, 0), (identity_columns, TILE)):
                    n = columns.shape[1]
                    pool.tensor_tensor(columns, bd_raw[:, at:at + n * SEQ].rearrange("p (e t) -> p e t", t=SEQ),
                                       ones[:, :, None].to_broadcast([P, n, SEQ]), ALU.mult).then_inc(mask_ready, 1)

            def whole_program(pair):
                if not pair:
                    place_mask_and_identity()
                split_bd(0, pair)
                split_a(1, pair)
                with pool.Fori(1, TILES - 1) as tile:
                    split_bd(tile, pair)
                    add_residual(tile - 1)
                    split_a(tile + 1, pair)
                split_bd(TILES - 1, pair)
                add_residual(TILES - 2)

            pool.memset(ones[:, :], 1.0).then_inc(ones_ready, 1)
            pool.memset(plan_columns, 0.0).then_inc(plan_cleared, 1)
            pool.wait_ge(ones_ready, 1)
            flag = pair_flag(pool)
            with pool.If(flag == 1):
                whole_program(True)
            with pool.Else():
                whole_program(False)

        @block.scalar
        def _(act):
            def split_hi_wgu(f):
                act.wait_ge(wgu_in[f % 2], 16 * (f // 2 + 1))
                nc.scalar.activation(wgu_chunk(0, f), stage_gu_chunk(f), ACT.Copy).then_inc(wgu_hi, 1)

            def split_hi_wd(f):
                w, n = WIDTHS[f], wd_turn(f)
                act.wait_ge(wd_in[n % 2], 16 * (n // 2 + 1))
                nc.scalar.activation(wd[0:w, 0, f, :], stage_d[0:w, n % 2, :], ACT.Copy).then_inc(wd_hi, 1)

            def split_hi_b(tile, f, pair):
                w = WIDTHS[f]
                at = 2 * STARTS[f]
                n = 2 * PAIR if pair else P
                act.wait_ge(b_in[f >= FIRST], 16 * b_piece_dmas(pair) * (tile + 1))
                if f >= 2:
                    act.wait_ge(up_done, FC * tile + f - 1)
                elif not (isinstance(tile, int) and tile == 0):
                    act.wait_ge(up_done, FC * tile - f)
                nc.scalar.activation(b_split[0:n, 0, f % 2, :, 0:w],
                                     b_raw[0:n, at:at + 2 * w].rearrange("p (g w) -> p g w", g=2), ACT.Copy
                                     ).then_inc(b_hi, 1)

            def normalise(tile, s):
                act.wait_ge(ascale_ready, SUBS * tile + s + 1)
                nc.scalar.activation(norm[:, s, :], ps_down[:, s, :], ACT.Copy, scale=rinv[:, s:s + 1]
                                     ).then_inc(norm_ready, 1)

            def split_hi_transposed(tile, s, ps_block):
                act.wait_ge(transposed, SUBS * tile + s + 1)
                if s > 0 or not (isinstance(tile, int) and tile == 0):
                    act.wait_ge(ffn_done, SUBS * tile + s)
                nc.scalar.activation(dt_split[:, 0, :, :], ps_block.rearrange("p (k t) -> p k t", k=KC),
                                     ACT.Copy).then_inc(dt_hi, 1)

            def split_hi_t(tile, pair):
                act.wait_ge(t_masked, tile + 1)
                if not pair:
                    nc.scalar.activation(t_split[:, 0, :, :], t_psum, ACT.Copy).then_inc(t_hi, 1)
                    return
                for first_row, done in ((0, t_hi), (2 * PAIR, t_hi_again)):
                    nc.scalar.activation(t_split[first_row:first_row + PAIR, 0, :, :], t_full, ACT.Copy
                                         ).then_inc(done, 1)

            def copy_first_gate(tile, first):
                act.wait_ge(t_done, tile + 1)
                if not first:
                    act.wait_ge(act_lo, FC * tile)
                nc.scalar.activation(act_full[0:FIRST_WIDTH, 0, :], ps_gate[0:FIRST_WIDTH, 0, 0:TILE], ACT.Copy
                                     ).then_inc(gate_copied, 1)

            def copy_first_up(tile, first):
                if not first:
                    act.wait_ge(act_done, FC * (tile - 1) + 1)
                nc.scalar.activation(up_full, ps_up[0:FIRST_WIDTH, 0, 0:TILE], ACT.Copy).then_inc(up_copied, 1)

            def copy_down_lora(tile):
                act.wait_ge(td_done, FC * (tile + 1))
                nc.scalar.activation(td_lo_part, ps_td[PAIR:2 * PAIR, 0:TILE], ACT.Copy).then_inc(td_copied, 1)

            def split_hi_down_lora(tile):
                act.wait_ge(td_masked, tile + 1)
                for first_row, done in ((0, td_hi), (2 * PAIR, td_hi_again)):
                    nc.scalar.activation(td_split[first_row:first_row + PAIR, 0, :], td_full, ACT.Copy
                                         ).then_inc(done, 1)

            def silu_gate(tile, f, first, pair):
                w = WIDTHS[f]
                if pair and f == 0:
                    act.wait_ge(gate_summed, tile + 1)
                    nc.scalar.activation(act_full[0:w, 0, :], act_full[0:w, 0, :], ACT.Silu).then_inc(silu_done, 1)
                    return
                act.wait_ge(gate_done, FC * tile + f + 1)
                if f >= 2:
                    act.wait_ge(act_lo, FC * tile + f - 1)
                elif not first:
                    act.wait_ge(act_lo, FC * tile - f)
                nc.scalar.activation(act_full[0:w, f % 2, :], ps_gate[0:w, f % 2, 0:TILE], ACT.Silu
                                     ).then_inc(silu_done, 1)

            def split_hi_act(tile, f, first):
                w = WIDTHS[f]
                act.wait_ge(act_done, FC * tile + f + 1)
                if f >= 2:
                    act.wait_ge(down_done, FC * tile + f - 1)
                elif not first:
                    act.wait_ge(down_done, FC * tile - f)
                nc.scalar.activation(act_split[0:w, 0, f % 2, :], act_full[0:w, f % 2, :], ACT.Copy
                                     ).then_inc(act_hi, 1)

            def run_tile(tile, first, pair):
                act.wait_ge(x_in, 16 * ENTRIES * (tile + 1))
                if not first:
                    act.wait_ge(up_done, FC * tile)
                nc.scalar.activation(xs_split(0), x_by_chunk, ACT.Copy).then_inc(x_hi, 1)
                if first:
                    load_wgu(act, 2)
                    load_wd(act, 0)
                    load_wd(act, 1)
                    if pair:
                        act.wait_ge(first_a_in, 32)
                    else:
                        act.wait_ge(a_in, a_loads(0, pair))
                    for k in range(KC):
                        nc.scalar.activation(a_split_chunk(0, k, loras(pair)), a_raw_chunk(k, loras(pair)),
                                             ACT.Copy).then_inc(a_hi, 1)
                    split_hi_wgu(2)
                    split_hi_wd(0)
                    split_hi_wd(1)
                else:
                    split_hi_act(tile - 1, FC - 1, False)
                split_hi_b(tile, 0, pair)
                split_hi_b(tile, 1, pair)
                if pair:
                    copy_first_gate(tile, first)
                if pair and not first:
                    copy_down_lora(tile - 1)
                split_hi_t(tile, pair)
                if pair and not first:
                    split_hi_down_lora(tile - 1)
                if pair:
                    copy_first_up(tile, first)
                for f in range(FC):
                    if first and 0 < f < FC - 1:
                        split_hi_wd(f + 1)
                    if first and 0 < f < FC - 2:
                        split_hi_wgu(f + 2)
                    silu_gate(tile, f, first, pair)
                    if not first and f == 2:
                        split_hi_transposed(tile - 1, 0, ps_misc[:, :])
                    if f < FC - 2:
                        split_hi_b(tile, f + 2, pair)
                    if not first and f == 1:
                        normalise(tile - 1, 1)
                    if f < FC - 1:
                        split_hi_act(tile, f, first)
                    if not first and f == 0:
                        normalise(tile - 1, 0)
                    if not first and f == 3:
                        split_hi_transposed(tile - 1, 1, ps_misc[:, :])

            act.wait_ge(ones_ready, 1)
            nc.scalar.activation(rinv[:, 0:1], ones[:, :], ACT.Silu).then_inc(table_ready, 1)
            for f in range(2):
                load_wgu(act, f)
            split_hi_wgu(0)
            split_hi_wgu(1)
            act.wait_ge(plan_steps, PLAN_ORDER_STEP)
            for e in range(1, ENTRIES, 2):
                load_x_entry(act, 0, e)
            load_a(act, lora_at(act, 0, ENTRIES - 1), 1, first_a_in)

            def whole_program(pair):
                run_tile(0, True, pair)
                with act.Fori(1, TILES) as tile:
                    run_tile(tile, False, pair)
                split_hi_act(TILES - 1, FC - 1, False)
                if pair:
                    copy_down_lora(TILES - 1)
                    split_hi_down_lora(TILES - 1)
                for s in range(SUBS):
                    normalise(TILES - 1, s)
                for s in range(SUBS):
                    split_hi_transposed(TILES - 1, s, ps_last[s])

            flag = pair_flag(act)
            with act.If(flag == 1):
                whole_program(True)
            with act.Else():
                whole_program(False)

        @block.vector
        def _(dve):
            def split_lo_wgu(f):
                dve.wait_ge(wgu_hi, f + 1)
                nc.vector.tensor_tensor(wgu_chunk(1, f), stage_gu_chunk(f), wgu_chunk(0, f).bitcast(F32),
                                        ALU.subtract).then_inc(wgu_lo, 1)

            def split_lo_wd(f):
                w, n = WIDTHS[f], wd_turn(f)
                dve.wait_ge(wd_hi, f + 1)
                nc.vector.tensor_tensor(wd[0:w, 1, f, :], stage_d[0:w, n % 2, :], wd[0:w, 0, f, :].bitcast(F32),
                                        ALU.subtract).then_inc(wd_lo, 1)

            def convert_wq(k):
                n = wq_turn(k)
                dve.wait_ge(wd_in[n % 2], 16 * (n // 2 + 1))
                nc.vector.tensor_scalar(wq[:, k, :], stage_d[:, n % 2, :].bitcast(I32), -1.5, None, ALU.add
                                        ).then_inc(wq_ready, 1)

            def split_lo_b(tile, f, pair):
                w = WIDTHS[f]
                at = 2 * STARTS[f]
                n = PAIR if pair else P
                lo = b_split[2 * PAIR:STACK, 0, f % 2, :, 0:w] if pair else b_split[:, 1, f % 2, :, 0:w]
                dve.wait_ge(b_hi, FC * tile + f + 1)
                nc.vector.tensor_tensor(lo, b_raw[0:n, at:at + 2 * w].rearrange("p (g w) -> p g w", g=2),
                                        b_split[0:n, 0, f % 2, :, 0:w].bitcast(F32), ALU.subtract
                                        ).then_inc(b_lo, 1)

            def split_ad(tile, f, pair):
                n = loras(pair)
                dve.wait_ge(ad_in[f >= FIRST], 16 * n * (tile + 1))
                if f >= 2:
                    dve.wait_ge(td_done, FC * tile + f - 1)
                elif not (isinstance(tile, int) and tile == 0):
                    dve.wait_ge(td_done, FC * tile - f)
                raw = ad_raw[:, 0:n, f * RANK:(f + 1) * RANK]
                hi, lo = (ad_split_chunk(part, f % 2, n).rearrange("p (e r) -> p e r", e=n) for part in range(2))
                nc.vector.tensor_copy(hi, raw).then_inc(ad_hi, 1)
                dve.wait_ge(ad_hi, FC * tile + f + 1)
                nc.vector.tensor_tensor(lo, raw, hi.bitcast(F32), ALU.subtract).then_inc(ad_ready, 1)

            def block_scales(tile, s):
                done = 2 * (SUBS * tile + s)
                dve.wait_ge(blocks_done, SUBS * tile + s + 1)
                nc.vector.tensor_reduce(amax[:, s:s + 1], ps_down[:, s, :], AX_X, ALU.max,
                                        apply_absolute_value=True).then_inc(amax_steps, 1)
                dve.wait_ge(amax_steps, done + 1)
                nc.vector.tensor_scalar(amax[:, s:s + 1], amax[:, s:s + 1], EPS, None, ALU.max
                                        ).then_inc(amax_steps, 1)
                dve.wait_ge(amax_steps, done + 2)
                nc.vector.tensor_tensor(ascale[:, s:s + 1], amax[:, s:s + 1], wscale[:, :], ALU.mult
                                        ).then_inc(ffn_scaled, 1)
                nc.vector.reciprocal(rinv[:, s:s + 1], amax[:, s:s + 1]).then_inc(ascale_ready, 1)

            def split_lo_transposed(tile, s, ps_block):
                dve.wait_ge(dt_hi, SUBS * tile + s + 1)
                nc.vector.tensor_tensor(dt_split[:, 1, :, :], ps_block.rearrange("p (k t) -> p k t", k=KC),
                                        dt_split[:, 0, :, :].bitcast(F32), ALU.subtract).then_inc(dt_lo, 1)

            def mask_t(tile, pair):
                dve.wait_ge(t_done, tile + 1)
                if pair:
                    dve.wait_ge(mask_gu_in, 16 * (tile + 1))
                    for g, ps_g in enumerate((ps_gate, ps_up)):
                        last = nc.vector.tensor_tensor(t_full[:, g, :], ps_g[FIRST_WIDTH:P, 0, 0:TILE], mask_gu,
                                                       ALU.mult)
                    last.then_inc(t_masked, 1)
                else:
                    t_entries = t_psum.rearrange("p g (e t) -> p g e t", e=ENTRIES)
                    nc.vector.tensor_tensor(t_entries, t_entries,
                                            block_mask.unsqueeze(1).to_broadcast([P, 2, ENTRIES, SEQ]), ALU.mult
                                            ).then_inc(t_masked, 1)

            def split_lo_t(tile, pair):
                dve.wait_ge(t_hi, tile + 1)
                if pair:
                    nc.vector.tensor_tensor(t_split[PAIR:2 * PAIR, 0, :, :], t_full,
                                            t_split[0:PAIR, 0, :, :].bitcast(F32), ALU.subtract).then_inc(t_lo, 1)
                else:
                    nc.vector.tensor_tensor(t_split[:, 1, :, :], t_psum, t_split[:, 0, :, :].bitcast(F32),
                                            ALU.subtract).then_inc(t_lo, 1)

            def mask_down_lora(tile, pair):
                if pair:
                    dve.wait_ge(td_copied, tile + 1)
                    nc.vector.tensor_tensor(td_full, ps_td[0:PAIR, 0:TILE], td_lo_part, ALU.add
                                            ).then_inc(td_summed, 1)
                    dve.wait_ge(td_summed, tile + 1)
                    dve.wait_ge(mask_d_in, 16 * (tile + 1))
                    nc.vector.tensor_tensor(td_full, td_full, mask_d, ALU.mult).then_inc(td_masked, 1)
                else:
                    dve.wait_ge(td_done, FC * (tile + 1))
                    td_entries = td_psum.rearrange("p (e t) -> p e t", e=ENTRIES)
                    nc.vector.tensor_tensor(td_entries, td_entries, block_mask, ALU.mult).then_inc(td_masked, 1)

            def split_lo_down_lora(tile, pair):
                if pair:
                    dve.wait_ge(td_hi, tile + 1)
                    nc.vector.tensor_tensor(td_split[PAIR:2 * PAIR, 0, :], td_full,
                                            td_split[0:PAIR, 0, :].bitcast(F32), ALU.subtract).then_inc(td_ready, 1)
                else:
                    dve.wait_ge(td_masked, tile + 1)
                    nc.vector.tensor_copy(td_split[:, 0, :], td_psum).then_inc(td_hi, 1)
                    dve.wait_ge(td_hi, tile + 1)
                    nc.vector.tensor_tensor(td_split[:, 1, :], td_psum, td_split[:, 0, :].bitcast(F32),
                                            ALU.subtract).then_inc(td_ready, 1)

            def scale_and_bias(tile, s, ps_block):
                dve.wait_ge(xres_in, 16 * ENTRIES * (tile + 1))
                dve.wait_ge(ffn_scaled, SUBS * (tile + 1))
                dve.wait_ge(ffn_done, SUBS * tile + s + 1)
                nc.vector.scalar_tensor_tensor(out_rows[:, s, :], ps_block, ascale[:, s:s + 1], bias[:, :],
                                               ALU.mult, ALU.add).then_inc(ffn_biased, 1)

            def add_first_lora(tile):
                gate_full = act_full[0:FIRST_WIDTH, 0, :]
                dve.wait_ge(gate_copied, tile + 1)
                dve.wait_ge(up_done, FC * tile + 1)
                nc.vector.tensor_tensor(gate_full, gate_full, first_lora[:, 0, :], ALU.add).then_inc(gate_summed, 1)
                dve.wait_ge(up_copied, tile + 1)
                nc.vector.tensor_tensor(up_full, up_full, first_lora[:, 1, :], ALU.add).then_inc(up_summed, 1)
                dve.wait_ge(silu_done, FC * tile + 1)
                dve.wait_ge(up_summed, tile + 1)
                nc.vector.tensor_tensor(gate_full, up_full, gate_full, ALU.mult).then_inc(act_done, 1)

            def gate_times_up(tile, f):
                w = WIDTHS[f]
                dve.wait_ge(silu_done, FC * tile + f + 1)
                dve.wait_ge(up_done, FC * tile + f + 1)
                nc.vector.tensor_tensor(act_full[0:w, f % 2, :], ps_up[0:w, f % 2, 0:TILE],
                                        act_full[0:w, f % 2, :], ALU.mult).then_inc(act_done, 1)

            def split_lo_act(tile, f):
                w = WIDTHS[f]
                dve.wait_ge(act_hi, FC * tile + f + 1)
                nc.vector.tensor_tensor(act_split[0:w, 1, f % 2, :], act_full[0:w, f % 2, :],
                                        act_split[0:w, 0, f % 2, :].bitcast(F32), ALU.subtract).then_inc(act_lo, 1)

            def run_tile(tile, first, pair):
                dve.wait_ge(x_hi, tile + 1)
                nc.vector.tensor_tensor(xs_split(1), x_by_chunk, xs_split(0).bitcast(F32), ALU.subtract
                                        ).then_inc(x_lo, 1)
                if first:
                    for k in range(KC):
                        dve.wait_ge(a_hi, k + 1)
                        last = nc.vector.tensor_tensor(a_split_chunk(1, k, loras(pair)),
                                                       a_raw_chunk(k, loras(pair)),
                                                       a_split_chunk(0, k, loras(pair)).bitcast(F32), ALU.subtract)
                    last.then_inc(a_ready, 1)
                    split_lo_wgu(2)
                    split_lo_wd(0)
                    split_lo_wd(1)
                    if not pair:
                        dve.wait_ge(mask_ready, 2)
                else:
                    split_lo_act(tile - 1, FC - 1)
                split_lo_b(tile, 0, pair)
                split_lo_b(tile, 1, pair)
                mask_t(tile, pair)
                if not first:
                    mask_down_lora(tile - 1, pair)
                split_lo_t(tile, pair)
                if not first:
                    split_lo_down_lora(tile - 1, pair)
                split_ad(tile, 0, pair)
                for f in range(FC):
                    if first and 0 < f < FC - 1:
                        split_lo_wd(f + 1)
                        if f + 1 >= WQ_FROM:
                            convert_wq(f + 1 - WQ_FROM)
                    if first and 0 < f < FC - 2:
                        split_lo_wgu(f + 2)
                    if not first and f == 2:
                        split_lo_transposed(tile - 1, 0, ps_misc[:, :])
                    if pair and f == 0:
                        add_first_lora(tile)
                    else:
                        gate_times_up(tile, f)
                    if not first and f == 0:
                        block_scales(tile - 1, 0)
                    if f < FC - 2:
                        split_lo_b(tile, f + 2, pair)
                    if not first and f == 0:
                        block_scales(tile - 1, 1)
                    if f < FC - 1:
                        split_lo_act(tile, f)
                        split_ad(tile, f + 1, pair)
                    if not first and f == 3:
                        split_lo_transposed(tile - 1, 1, ps_misc[:, :])
                    if not first and f in (2, 4):
                        scale_and_bias(tile - 1, f // 2 - 1, ps_misc[:, :])
                if first:
                    dve.wait_ge(const_in, 48 if pair else 32)

            def make_plan():
                step = [0]

                def then(instruction):
                    instruction.then_inc(plan_steps, 1)
                    step[0] += 1
                    dve.wait_ge(plan_steps, step[0])

                tt, ts, red = nc.vector.tensor_tensor, nc.vector.tensor_scalar, nc.vector.tensor_reduce
                dve.wait_ge(index_in, 32)
                dve.wait_ge(plan_cleared, 1)
                then(nc.vector.scalar_tensor_tensor(keys, idx_places, float(BATCH), number_places, ALU.mult, ALU.add))
                then(ts(compared, keys[:, 0:BATCH], keys[:, BATCH:BATCH + 1], None, ALU.is_lt))
                then(red(rank_col, compared, AX_X, ALU.add))
                then(ts(one_hot, number_places[:, 0:BATCH], rank_col, None, ALU.is_equal))
                then(ts(run_key, idx_places[:, BATCH:BATCH + 1], float(BATCH), BATCH - 0.5, ALU.mult, ALU.add))
                then(ts(compared, keys[:, 0:BATCH], run_key, None, ALU.is_lt))
                then(red(plan_columns[:, 64:65], compared, AX_X, ALU.add))
                nc.vector.tensor_copy(plan_columns[:, 32:33], idx_places[:, BATCH:BATCH + 1])
                then(nc.vector.tensor_copy(plan_columns[:, 0:1], number_places[:, BATCH:BATCH + 1]))
                dve.wait_ge(plan_gathered, 1)
                for source, first_row in ((0, 0), (32, 64)):
                    by_half = ps_plan[source:source + 1, :].rearrange("p (t h e) -> p t h e", t=TILES, h=2)
                    for half in range(2):
                        row = first_row + 32 * half
                        nc.vector.tensor_copy(plan[row:row + 1, 0:BATCH // 2]
                                              .rearrange("p (t e) -> p t e", t=TILES), by_half[:, :, half, :])
                then(nc.vector.tensor_copy(sorted_idx, ps_plan[32:33, :]))
                then(tt(tile_rows[64:65, :], ps_plan[64:65, 0:BATCH:ENTRIES],
                        number_places[64:65, 0:BATCH:ENTRIES], ALU.subtract))
                ts(plan_run, tile_rows[64:65, :], float(ENTRIES), None, ALU.min)
                now = ps_plan[32:33, :].rearrange("p (t e) -> p t e", e=ENTRIES)[:, :, 0:ENTRIES - 1]
                following = sorted_idx.rearrange("p (t e) -> p t e", e=ENTRIES)[:, :, 1:ENTRIES]
                then(tt(changes, now, following, ALU.not_equal))
                then(red(tile_rows[32:33, :], changes, AX_X, ALU.add))
                then(red(most_changes, tile_rows[32:33, :], AX_X, ALU.max))
                ts(plan_flag, most_changes, 1.0, None, ALU.is_le).then_inc(plan_ready, 1)

            def whole_program(pair):
                run_tile(0, True, pair)
                with dve.Fori(1, TILES) as tile:
                    run_tile(tile, False, pair)
                split_lo_act(TILES - 1, FC - 1)
                mask_down_lora(TILES - 1, pair)
                split_lo_down_lora(TILES - 1, pair)
                for s in range(SUBS):
                    block_scales(TILES - 1, s)
                split_lo_transposed(TILES - 1, 0, ps_last[0])
                scale_and_bias(TILES - 1, 0, ps_last[0])
                split_lo_transposed(TILES - 1, 1, ps_last[1])
                dve.wait_ge(ffn_biased, SUBS * TILES - 1)
                nc.vector.tensor_tensor(out_rows[:, 0, :], x_res[:, 0, :], out_rows[:, 0, :], ALU.add
                                        ).then_inc(out_ready, 1)
                scale_and_bias(TILES - 1, 1, ps_last[1])
                dve.wait_ge(ffn_biased, SUBS * TILES)
                nc.vector.tensor_tensor(out_rows[:, 1, :], x_res[:, 1, :], out_rows[:, 1, :], ALU.add
                                        ).then_inc(out_ready, 1)

            make_plan()
            split_lo_wgu(0)
            split_lo_wgu(1)
            flag = pair_flag(dve)
            with dve.If(flag == 1):
                whole_program(True)
            with dve.Else():
                whole_program(False)

        @block.tensor
        def _(pe):
            HI, LO = 0, 1
            PASSES = [(HI, HI), (LO, HI), (HI, LO)]

            def lora_a(tile):
                pe.wait_ge(a_ready, tile + 1)
                for g in range(2):
                    for n, (ws, xp) in enumerate(PASSES):
                        for k in range(KC):
                            last = nc.tensor.matmul(ps_misc[:, g * TILE:(g + 1) * TILE],
                                                    a_split[:, ws, k, g * P:(g + 1) * P], xs[:, xp, k, :],
                                                    start=(n == 0 and k == 0), stop=(n == 2 and k == KC - 1))
                last.then_inc(t_done, 1)

            def main_pass(ps_out, f, g, ws, xp, start=False, with_a=False, stop=False):
                m = P if with_a else WIDTHS[f]
                for k in range(KC):
                    w = wgu_first[:, ws, k, g, 0:m] if f == 0 else wgu_chunk(ws, f)[:, k, g, :]
                    last = nc.tensor.matmul(ps_out[0:m, f % 2, 0:TILE], w, xs[:, xp, k, :],
                                            start=(start and k == 0), stop=(stop and k == KC - 1))
                return last

            def project_main(ps_out, f, g, passes=(0, 1, 2)):
                for n in passes:
                    main_pass(ps_out, f, g, *PASSES[n], n == 0)

            def first_chunk_main(tile, first, pair):
                if not first:
                    pe.wait_ge(act_done, FC * tile)
                else:
                    pe.wait_ge(wgu_hi, 1)
                    pe.wait_ge(wgu_lo, 1)
                pe.wait_ge(x_hi, tile + 1)
                if pair:
                    pe.wait_ge(a_ready, tile + 1)
                order = [(HI, HI), (LO, HI), (HI, LO)]
                for n, (ws, xp) in enumerate(order):
                    if xp == LO:
                        pe.wait_ge(x_lo, tile + 1)
                    main_pass(ps_gate, 0, 0, ws, xp, n == 0, pair, pair and n == 2)
                    last = main_pass(ps_up, 0, 1, ws, xp, n == 0, pair, pair and n == 2)
                if pair:
                    last.then_inc(t_done, 1)
                else:
                    lora_a(tile)

            def project_lora(ps_out, f, g, done, pair):
                w = WIDTHS[f]
                if pair and f == 0:
                    last = nc.tensor.matmul(first_lora[:, g, :], b_split[0:STACK, 0, 0, g, 0:w],
                                            t_split[0:STACK, 0, g, :], start=True, stop=True)
                elif pair:
                    last = nc.tensor.matmul(ps_out[0:w, f % 2, 0:TILE], b_split[0:STACK, 0, f % 2, g, 0:w],
                                            t_split[0:STACK, 0, g, :], start=False, stop=True)
                else:
                    for n, (ws, tp) in enumerate(PASSES):
                        last = nc.tensor.matmul(ps_out[0:w, f % 2, 0:TILE], b_split[:, ws, f % 2, g, 0:w],
                                                t_split[:, tp, g, :], start=False, stop=(n == 2))
                last.then_inc(done, 1)

            def slots_free(tile, f, first):
                if f >= 2:
                    pe.wait_ge(act_done, FC * tile + f - 1)
                elif not first:
                    pe.wait_ge(act_done, FC * tile - f)
                if first:
                    pe.wait_ge(wgu_lo, f + 1)

            def gate(tile, f, first, pair):
                slots_free(tile, f, first)
                project_main(ps_gate, f, 0)
                pe.wait_ge(b_lo, FC * tile + f + 1)
                project_lora(ps_gate, f, 0, gate_done, pair)

            def add_lora(tile, f, pair):
                pe.wait_ge(t_lo, tile + 1)
                if pair:
                    pe.wait_ge(t_hi_again, tile + 1)
                pe.wait_ge(b_lo, FC * tile + f + 1)
                project_lora(ps_gate, f, 0, gate_done, pair)
                project_lora(ps_up, f, 1, up_done, pair)

            def lora_a_down(tile, f, pair):
                w = WIDTHS[f]
                pe.wait_ge(ad_ready, FC * tile + f + 1)
                pe.wait_ge(act_lo, FC * tile + f + 1)
                if pair:
                    for part in ((HI, LO) if f == 0 else (LO, HI)):
                        m = 2 * PAIR if part == HI else PAIR
                        last = nc.tensor.matmul(ps_td[0:m, 0:TILE], ad_split[0:w, f % 2, 0:m],
                                                act_split[0:w, part, f % 2, :], start=(f == 0 and part == HI),
                                                stop=(f == FC - 1 and part == HI))
                else:
                    for n, (ws, ap) in enumerate(PASSES):
                        last = nc.tensor.matmul(ps_td[:, 0:TILE], ad_split[0:w, f % 2, ws * P:(ws + 1) * P],
                                                act_split[0:w, ap, f % 2, :],
                                                start=(f == 0 and n == 0), stop=(f == FC - 1 and n == 2))
                last.then_inc(td_done, 1)

            def down(tile, f, first):
                w = WIDTHS[f]
                if first:
                    pe.wait_ge(wd_lo, f + 1)
                elif f == 0:
                    pe.wait_ge(norm_ready, SUBS * tile)
                for s in range(SUBS):
                    for n, (ap, wp) in enumerate(PASSES):
                        last = nc.tensor.matmul(ps_down[:, s, :], act_split[0:w, ap, f % 2, s * P:(s + 1) * P],
                                                wd[0:w, wp, f, :], start=(f == 0 and n == 0), stop=False)
                last.then_inc(down_done, 1)

            def lora_b_down(tile, pair):
                pe.wait_ge(bd_ready, tile + 1)
                pe.wait_ge(td_ready, tile + 1)
                if pair:
                    pe.wait_ge(td_hi_again, tile + 1)
                for s in range(SUBS):
                    if pair:
                        last = nc.tensor.matmul(ps_down[:, s, :], td_split[0:STACK, 0, s * P:(s + 1) * P],
                                                bd_split[0:STACK, 0, :], start=False, stop=True)
                    else:
                        for n, (tp, bp) in enumerate(PASSES):
                            last = nc.tensor.matmul(ps_down[:, s, :], td_split[:, tp, s * P:(s + 1) * P],
                                                    bd_split[:, bp, :], start=False, stop=(n == 2))
                    last.then_inc(blocks_done, 1)

            def transpose_block(tile, s, ps_block, pair):
                pe.wait_ge(norm_ready, SUBS * tile + s + 1)
                for k in range(KC):
                    last = nc.tensor.transpose(ps_block[:, k * P:(k + 1) * P], norm[:, s, k * P:(k + 1) * P],
                                               pair_identity if pair else general_identity)
                last.then_inc(transposed, 1)

            def ffn_block(tile, s, ps_block):
                pe.wait_ge(wq_ready, KC)
                pe.wait_ge(dt_lo, SUBS * tile + s + 1)
                for part in (HI, LO):
                    for k in range(KC):
                        last = nc.tensor.matmul(ps_block, dt_split[:, part, k, :], wq[:, k, :],
                                                start=(part == HI and k == 0), stop=(part == LO and k == KC - 1))
                last.then_inc(ffn_done, 1)

            def run_tile(tile, first, pair):
                first_chunk_main(tile, first, pair)
                if not first:
                    last_down(tile - 1, pair)
                slots_free(tile, 1, first)
                project_main(ps_gate, 1, 0)
                project_main(ps_up, 1, 1, (0,))
                add_lora(tile, 0, pair)
                if not first:
                    lora_b_down(tile - 1, pair)
                project_main(ps_up, 1, 1, (1, 2))
                add_lora(tile, 1, pair)
                for f in range(2, FC):
                    gate(tile, f, first, pair)
                    project_main(ps_up, f, 1)
                    if f == 2:
                        lora_a_down(tile, 0, pair)
                        down(tile, 0, first)
                        if not first:
                            transpose_block(tile - 1, 0, ps_misc[:, :], pair)
                    project_lora(ps_up, f, 1, up_done, pair)
                    lora_a_down(tile, f - 1, pair)
                    down(tile, f - 1, first)
                    if not first and f == 3:
                        pe.wait_ge(ffn_biased, SUBS * tile - 1)
                        transpose_block(tile - 1, 1, ps_misc[:, :], pair)
                    if not first and f in (2, 4):
                        ffn_block(tile - 1, f // 2 - 1, ps_misc[:, :])

            def last_down(tile, pair):
                lora_a_down(tile, FC - 1, pair)
                down(tile, FC - 1, False)

            def whole_program(pair):
                run_tile(0, True, pair)
                with pe.Fori(1, TILES) as tile:
                    run_tile(tile, False, pair)
                last_down(TILES - 1, pair)
                lora_b_down(TILES - 1, pair)
                for s in range(SUBS):
                    transpose_block(TILES - 1, s, ps_last[s], pair)
                for s in range(SUBS):
                    ffn_block(TILES - 1, s, ps_last[s])

            pe.wait_ge(plan_steps, PLAN_COLUMNS_STEP)
            nc.tensor.matmul(ps_plan, plan_columns, one_hot, start=True, stop=True).then_inc(plan_gathered, 1)
            flag = pair_flag(pe)
            with pe.If(flag == 1):
                whole_program(True)
            with pe.Else():
                whole_program(False)


def kernel(x, itok_B_2_6, L0_cond_W_gate, L0_cond_W_up, L0_cond_W_down, L0_cond_A_gate, L0_cond_B_gate,
           L0_cond_A_up, L0_cond_B_up, L0_cond_A_down, L0_cond_B_down, L0_ffn_weight_2bit, L0_ffn_weight_scale,
           L0_ffn_bias):
    import concourse.bacc as bacc
    from concourse.bass_utils import run_bass_kernel_spmd

    a = np.asarray
    x_tok = a(x).reshape(BATCH, SEQ, H)
    x_feat = x_tok.reshape(BATCH, SEQ, KC, P).transpose(0, 3, 2, 1).reshape(BATCH, P, KC * SEQ)

    def by_chunk(gate, up):
        return [np.stack([gate[..., a:b], up[..., a:b]], axis=-2) for a, b in zip(STARTS, STARTS[1:])]

    wt = [a(w).T.reshape(KC, P, FF).transpose(1, 0, 2) for w in (L0_cond_W_gate, L0_cond_W_up)]
    w_gu = np.concatenate([c.reshape(P, -1) for c in by_chunk(*wt)], axis=1)
    w_down = a(L0_cond_W_down).T
    w_2bit = a(L0_ffn_weight_2bit).T.reshape(KC, P, H).transpose(1, 0, 2)
    a_gu = np.stack([a(m)[0].reshape(LORAS, RANK, KC, P).transpose(0, 3, 2, 1)
                     for m in (L0_cond_A_gate, L0_cond_A_up)], axis=3).reshape(LORAS, P, AGU)
    a_down = np.zeros((LORAS, P, FC, RANK), a(L0_cond_A_down).dtype)
    for f, w in enumerate(WIDTHS):
        a_down[:, :w, f, :] = a(L0_cond_A_down)[0, :, :, STARTS[f]:STARTS[f + 1]].transpose(0, 2, 1)
    a_down = a_down.reshape(LORAS, P, FC * RANK)
    bt = [a(m)[0].transpose(0, 2, 1) for m in (L0_cond_B_gate, L0_cond_B_up, L0_cond_B_down)]
    b_rows = np.concatenate([c.reshape(LORAS, RANK, -1) for c in by_chunk(bt[0], bt[1])] + [bt[2]], axis=2)
    scale_col = np.broadcast_to(a(L0_ffn_weight_scale).reshape(1, 1), (P, 1))
    bias_rows = np.broadcast_to(a(L0_ffn_bias).reshape(1, H), (P, H))
    entry_of_row = np.arange(P)[:, None] // RANK
    entry_of_token = np.arange(TILE)[None, :] // SEQ
    block_mask = np.where(entry_of_row == entry_of_token, SCALE, 0.0).astype(np.float32)
    identity = np.eye(P, dtype=np.float32)
    index = a(itok_B_2_6).reshape(-1)
    index_rows = np.concatenate([np.broadcast_to(index, (P, BATCH)), index[:, None]], axis=1)
    number = np.arange(BATCH, dtype=np.float32)
    places = np.concatenate([np.broadcast_to(number, (P, BATCH)), number[:, None]], axis=1)
    second_row = np.arange(PAIR)[None, :, None] // RANK
    second_token = entry_of_token[None] >= np.arange(ENTRIES + 1)[:, None, None]
    pair_masks = np.where(second_row == second_token, SCALE, 0.0).astype(np.float32)

    nc = bacc.Bacc("TRN2", target_bir_lowering=False, num_devices=1, dynamic_dma_scratch_size=1024)
    arrays, args = {}, []
    for name, v in [("x_tok", x_tok), ("x_feat", x_feat), ("lora_index", index_rows),
                    ("places", places), ("pair_masks", pair_masks), ("w_gu", w_gu),
                    ("w_down", w_down), ("w_2bit", w_2bit), ("a_gu", a_gu), ("a_down", a_down),
                    ("b_rows", b_rows), ("scale_col", scale_col), ("bias_rows", bias_rows),
                    ("block_mask_in", block_mask), ("identity_in", identity)]:
        v = np.ascontiguousarray(v)
        arrays[name] = v
        args.append(nc.dram_tensor(name, v.shape, mybir.dt.from_np(v.dtype), kind="ExternalInput").ap())
    args.append(nc.dram_tensor("out", (BATCH, SEQ, H), F32, kind="ExternalOutput").ap())
    build(nc, *args)
    result = run_bass_kernel_spmd(nc, [arrays], core_ids=[0])
    return result.results[0]["out"].reshape(x.shape)
```
